# Optimizing a Trainium2 kernel written in Bass

```python
import numpy as np
import jax
import jax.numpy as jnp

def _softmax(x, axis=-1):
    return jax.nn.softmax(x, axis=axis)

def _gelu(x):
    return jax.nn.gelu(x, approximate=True)

def _silu(x):
    return jax.nn.silu(x)

def _sigmoid(x):
    return jax.nn.sigmoid(x)

def _layernorm(x, axis=-1, eps=1e-05):
    m = jnp.mean(x, axis=axis, keepdims=True)
    v = jnp.var(x, axis=axis, keepdims=True)
    return (x - m) / jnp.sqrt(v + eps)

def _scatter_add(tgt, idx, src, axis=0):
    return tgt.at[idx].add(src)

def _segment_sum(src, seg, n):
    return jax.ops.segment_sum(src, seg, n)
kernel_name = 'mk_adaln_ffn_d4_seqx_r4_5f46fe'

def setup_inputs(seed: int=0):
    np.random.seed(seed)
    _w = jnp.asarray

    def _rec_inputs():
        import jax
        import jax.numpy as jnp
        _rk = jax.random.key(seed)
        x = -0.0003929 + 0.9999 * jax.random.normal(jax.random.fold_in(_rk, 1), (2, 1024, 256), jnp.float32)
        _lenS = 1024 - jax.random.randint(jax.random.fold_in(_rk, 7), (2,), 0, max(1, 1024 // 4) + 1, jnp.int32)
        _lenS2 = 1024 - jax.random.randint(jax.random.fold_in(_rk, 8), (2,), 0, max(1, 1024 // 4) + 1, jnp.int32)
        cond_1024 = 0.00061147 + 0.102565 * jax.random.normal(jax.random.fold_in(_rk, 11), (2, 256), jnp.float32)
        return (x, cond_1024)
    x, cond_1024 = _rec_inputs()

    def _L0_cond_setup():
        import jax, jax.numpy as jnp
        import numpy as np
        key = jax.random.key(seed)
        ks = jax.random.split(key, 8)
        B, L, D, N, K = (4, 1024, 256, 64, 4)
        return {'x': jax.random.normal(ks[0], (B, L, D), dtype=jnp.float32), 'conv_w': jax.random.normal(ks[1], (K, 1, D), dtype=jnp.float32) * 0.1, 'conv_b': jnp.zeros((D,), dtype=jnp.float32), 'Wp': jax.random.normal(ks[2], (D, 2 * N), dtype=jnp.float32) * (1.0 / np.sqrt(D)), 'bp': jnp.zeros((2 * N,), dtype=jnp.float32), 'Ws': jax.random.normal(ks[3], (D, N), dtype=jnp.float32) * (1.0 / np.sqrt(D)), 'bs': jnp.zeros((N,), dtype=jnp.float32), 'A_log': jax.random.normal(ks[4], (N,), dtype=jnp.float32) * 0.02, 'dt_log': jax.random.normal(ks[5], (N,), dtype=jnp.float32) * 0.02, 'Wo': jax.random.normal(ks[6], (N, D), dtype=jnp.float32) * (1.0 / np.sqrt(N)), 'bo': jnp.zeros((D,), dtype=jnp.float32)}
    _L0_cond_all = _L0_cond_setup()
    _L0_cond_in = {k: v for k, v in _L0_cond_all.items() if k in ('conv_b', 'Wp', 'bp', 'Ws', 'bs', 'A_log', 'dt_log', 'Wo', 'bo')}
    del _L0_cond_all

    def _L0_ffn_setup():
        import jax, jax.numpy as jnp
        import numpy as np
        B, N, D = (4, 512, 256)
        SPARSITY = 0.01
        key = jax.random.key(seed)
        k1, k2, k3 = jax.random.split(key, 3)
        x = jax.random.normal(k1, (B, N, D), dtype=jnp.float32)
        spatial = jax.random.normal(k2, (D, D), dtype=jnp.float32) * 0.02
        freq = jnp.fft.fft(spatial, axis=-1)
        k = int(D * SPARSITY)
        mag = jnp.abs(freq)
        kth = jax.lax.top_k(mag, k)[0][:, -1:]
        w_sparse = jnp.where(mag >= kth, freq, 0.0 + 0j)
        bias = jax.random.normal(k3, (D,), dtype=jnp.float32) * 0.01
        return {'x': x, 'w_freq_real': jnp.real(w_sparse).astype(jnp.float32), 'w_freq_imag': jnp.imag(w_sparse).astype(jnp.float32), 'bias': bias}
    _L0_ffn_all = _L0_ffn_setup()
    _L0_ffn_in = {k: v for k, v in _L0_ffn_all.items() if k in ('w_freq_real', 'w_freq_imag', 'bias')}
    del _L0_ffn_all

    def _L1_cond_setup():
        import jax, jax.numpy as jnp
        import numpy as np
        LATENT = 256
        key = jax.random.key(seed)
        k1, k2, k3, k4 = jax.random.split(key, 4)
        B, T, D = (64, 128, LATENT)
        h_t = jax.random.normal(k1, (B, D), dtype=jnp.float32)
        z = jax.random.normal(k2, (B, T, D), dtype=jnp.float32)
        bound = 1.0 / np.sqrt(2 * D)
        W = jax.random.uniform(k3, (D, 2 * D), minval=-bound, maxval=bound, dtype=jnp.float32)
        b = jax.random.uniform(k4, (D,), minval=-bound, maxval=bound, dtype=jnp.float32)
        alpha = jnp.full((D,), 0.1, dtype=jnp.float32)
        return {'h_t': h_t, 'z': z, 'W': W, 'b': b, 'alpha': alpha}
    _L1_cond_all = _L1_cond_setup()
    _L1_cond_in = {k: v for k, v in _L1_cond_all.items() if k in ('W', 'b', 'alpha')}
    del _L1_cond_all

    def _L1_ffn_setup():
        import jax, jax.numpy as jnp
        import numpy as np
        HIDDEN = 256
        INNER = 1024

        def _weight_quant(w):
            scale = 1.0 / jnp.clip(jnp.mean(jnp.abs(w)), 1e-05)
            wq = jnp.clip(jnp.round(w * scale), -1.0, 1.0) / scale
            return w + jax.lax.stop_gradient(wq - w)

        def _act_quant(x):
            scale = 127.0 / jnp.clip(jnp.max(jnp.abs(x), axis=-1, keepdims=True), 1e-05)
            xq = jnp.clip(jnp.round(x * scale), -128.0, 127.0) / scale
            return x + jax.lax.stop_gradient(xq - x)

        def _bitlinear(x, w):
            return jnp.einsum('bsi,oi->bso', _act_quant(x), _weight_quant(w))
        key = jax.random.key(seed)
        k0, k1, k2, k3 = jax.random.split(key, 4)
        x = jax.random.normal(k0, (4, 512, HIDDEN), dtype=jnp.float32)
        w_gate = jax.random.normal(k1, (INNER, HIDDEN), dtype=jnp.float32) / np.sqrt(HIDDEN)
        w_up = jax.random.normal(k2, (INNER, HIDDEN), dtype=jnp.float32) / np.sqrt(HIDDEN)
        w_down = jax.random.normal(k3, (HIDDEN, INNER), dtype=jnp.float32) / np.sqrt(INNER)
        return {'x': x, 'w_gate': w_gate, 'w_up': w_up, 'w_down': w_down}
    _L1_ffn_all = _L1_ffn_setup()
    _L1_ffn_in = {k: v for k, v in _L1_ffn_all.items() if k in ('w_gate', 'w_up', 'w_down')}
    del _L1_ffn_all

    def _L2_cond_setup():
        import jax, jax.numpy as jnp
        import numpy as np
        B, T, D_IN, V_IN, E = (64, 128, 256, 256, 256)
        key = jax.random.key(seed)
        ks = jax.random.split(key, 16)
        s = 0.01
        return {'video': jax.random.normal(ks[0], (B, V_IN), jnp.float32), 'seq': jax.random.normal(ks[1], (B, T, D_IN), jnp.float32), 'W_z': jax.random.normal(ks[2], (D_IN, E), jnp.float32) * s, 'U_z': jax.random.normal(ks[3], (E, E), jnp.float32) * s, 'C_z': jax.random.normal(ks[4], (V_IN, E), jnp.float32) * s, 'b_z': jnp.zeros((E,), jnp.float32), 'W_r': jax.random.normal(ks[5], (D_IN, E), jnp.float32) * s, 'U_r': jax.random.normal(ks[6], (E, E), jnp.float32) * s, 'C_r': jax.random.normal(ks[7], (V_IN, E), jnp.float32) * s, 'b_r': jnp.zeros((E,), jnp.float32), 'W': jax.random.normal(ks[8], (D_IN, E), jnp.float32) * s, 'U': jax.random.normal(ks[9], (E, E), jnp.float32) * s, 'C': jax.random.normal(ks[10], (V_IN, E), jnp.float32) * s, 'b': jnp.zeros((E,), jnp.float32)}
    _L2_cond_all = _L2_cond_setup()
    _L2_cond_in = {k: v for k, v in _L2_cond_all.items() if k in ('W_z', 'U_z', 'C_z', 'b_z', 'W_r', 'U_r', 'C_r', 'b_r', 'W', 'U', 'C', 'b')}
    del _L2_cond_all

    def _L2_ffn_setup():
        import jax, jax.numpy as jnp
        import numpy as np
        NUM_EXPERTS = 64
        TOP_K = 8
        HIDDEN = 256
        INTER = 192
        B, S = (2, 512)
        key = jax.random.key(seed)
        k1, k2, k3, k4 = jax.random.split(key, 4)
        hidden_states = jax.random.normal(k1, (B, S, HIDDEN), jnp.float32)
        gate = jax.random.normal(k2, (NUM_EXPERTS, HIDDEN), jnp.float32) * 0.02
        gate_up_proj = jax.random.normal(k3, (NUM_EXPERTS, 2 * INTER, HIDDEN), jnp.float32) * 0.02
        down_proj = jax.random.normal(k4, (NUM_EXPERTS, HIDDEN, INTER), jnp.float32) * 0.02
        return {'hidden_states': hidden_states, 'gate': gate, 'gate_up_proj': gate_up_proj, 'down_proj': down_proj}
    _L2_ffn_all = _L2_ffn_setup()
    _L2_ffn_in = {k: v for k, v in _L2_ffn_all.items() if k in ('gate', 'gate_up_proj', 'down_proj')}
    del _L2_ffn_all

    def _L3_cond_setup():
        import jax, jax.numpy as jnp
        import numpy as np
        TOP_K = 2
        N_EXPERTS = 8
        N_SHARED = 1
        EPS = 1e-09
        key = jax.random.key(seed)
        ks = jax.random.split(key, 10)
        B, T, d = (2, 512, 256)
        h_s, h_r, E = (512, 128, N_EXPERTS)
        return {'x': jax.random.normal(ks[0], (B, T, d), jnp.float32), 't_emb': jax.random.normal(ks[1], (B, d), jnp.float32), 'router_w': jax.random.normal(ks[2], (E, d), jnp.float32) * 0.01, 'router_t_w': jax.random.normal(ks[3], (E, d), jnp.float32) * 0.01, 'router_bias': jnp.zeros((E,), jnp.float32), 'sw1': jax.random.normal(ks[4], (h_s, d), jnp.float32) * 0.02, 'sw3': jax.random.normal(ks[5], (h_s, d), jnp.float32) * 0.02, 'sw2': jax.random.normal(ks[6], (d, h_s), jnp.float32) * 0.02, 'rw1': jax.random.normal(ks[7], (E, h_r, d), jnp.float32) * 0.02, 'rw2': jax.random.normal(ks[8], (E, d, h_r), jnp.float32) * 0.02}
    _L3_cond_all = _L3_cond_setup()
    _L3_cond_in = {k: v for k, v in _L3_cond_all.items() if k in ('router_w', 'router_t_w', 'router_bias', 'sw1', 'sw3', 'sw2', 'rw1', 'rw2')}
    del _L3_cond_all

    def _L3_ffn_setup():
        import jax, jax.numpy as jnp
        import numpy as np
        QMIN, QMAX = (-128.0, 127.0)

        def _affine_quantize(x):
            amin, amax = (jnp.min(x), jnp.max(x))
            scale = jnp.maximum((amax - amin) / 255.0, 1e-08)
            zp = jnp.clip(jnp.round(-amin / scale) + QMIN, QMIN, QMAX)
            q = jnp.clip(jnp.round(x / scale) + zp, QMIN, QMAX)
            return (q, scale, zp)

        def _sym_quantize(w):
            scale = jnp.maximum(jnp.max(jnp.abs(w)) / 127.0, 1e-08)
            q = jnp.clip(jnp.round(w / scale), -127.0, 127.0)
            return (q, scale)

        def _qlinear(x, W, b):
            xq, sx, zx = _affine_quantize(x)
            wq, sw = _sym_quantize(W)
            acc = jnp.einsum('bsh,oh->bso', xq - zx, wq)
            return acc * (sx * sw) + b
        key = jax.random.key(seed)
        k1, k2, k3, k4, k5 = jax.random.split(key, 5)
        d, h = (256, 1024)
        x = jax.random.normal(k1, (4, 1024, d), dtype=jnp.float32)
        W1 = jax.random.normal(k2, (h, d), dtype=jnp.float32) * (1.0 / np.sqrt(d))
        b1 = jax.random.normal(k3, (h,), dtype=jnp.float32) * 0.02
        W2 = jax.random.normal(k4, (d, h), dtype=jnp.float32) * (1.0 / np.sqrt(h))
        b2 = jax.random.normal(k5, (d,), dtype=jnp.float32) * 0.02
        return {'x': x, 'W1': W1, 'b1': b1, 'W2': W2, 'b2': b2}
    _L3_ffn_all = _L3_ffn_setup()
    _L3_ffn_in = {k: v for k, v in _L3_ffn_all.items() if k in ('W1', 'b1', 'W2', 'b2')}
    del _L3_ffn_all
    return {'x': x, 'cond_1024': cond_1024, 'L0_cond_conv_b': _L0_cond_in['conv_b'], 'L0_cond_Wp': _L0_cond_in['Wp'], 'L0_cond_bp': _L0_cond_in['bp'], 'L0_cond_Ws': _L0_cond_in['Ws'], 'L0_cond_bs': _L0_cond_in['bs'], 'L0_cond_A_log': _L0_cond_in['A_log'], 'L0_cond_dt_log': _L0_cond_in['dt_log'], 'L0_cond_Wo': _L0_cond_in['Wo'], 'L0_cond_bo': _L0_cond_in['bo'], 'L0_ffn_w_freq_real': _L0_ffn_in['w_freq_real'], 'L0_ffn_w_freq_imag': _L0_ffn_in['w_freq_imag'], 'L0_ffn_bias': _L0_ffn_in['bias'], 'L1_cond_W': _L1_cond_in['W'], 'L1_cond_b': _L1_cond_in['b'], 'L1_cond_alpha': _L1_cond_in['alpha'], 'L1_ffn_w_gate': _L1_ffn_in['w_gate'], 'L1_ffn_w_up': _L1_ffn_in['w_up'], 'L1_ffn_w_down': _L1_ffn_in['w_down'], 'L2_cond_W_z': _L2_cond_in['W_z'], 'L2_cond_U_z': _L2_cond_in['U_z'], 'L2_cond_C_z': _L2_cond_in['C_z'], 'L2_cond_b_z': _L2_cond_in['b_z'], 'L2_cond_W_r': _L2_cond_in['W_r'], 'L2_cond_U_r': _L2_cond_in['U_r'], 'L2_cond_C_r': _L2_cond_in['C_r'], 'L2_cond_b_r': _L2_cond_in['b_r'], 'L2_cond_W': _L2_cond_in['W'], 'L2_cond_U': _L2_cond_in['U'], 'L2_cond_C': _L2_cond_in['C'], 'L2_cond_b': _L2_cond_in['b'], 'L2_ffn_gate': _L2_ffn_in['gate'], 'L2_ffn_gate_up_proj': _L2_ffn_in['gate_up_proj'], 'L2_ffn_down_proj': _L2_ffn_in['down_proj'], 'L3_cond_router_w': _L3_cond_in['router_w'], 'L3_cond_router_t_w': _L3_cond_in['router_t_w'], 'L3_cond_router_bias': _L3_cond_in['router_bias'], 'L3_cond_sw1': _L3_cond_in['sw1'], 'L3_cond_sw3': _L3_cond_in['sw3'], 'L3_cond_sw2': _L3_cond_in['sw2'], 'L3_cond_rw1': _L3_cond_in['rw1'], 'L3_cond_rw2': _L3_cond_in['rw2'], 'L3_ffn_W1': _L3_ffn_in['W1'], 'L3_ffn_b1': _L3_ffn_in['b1'], 'L3_ffn_W2': _L3_ffn_in['W2'], 'L3_ffn_b2': _L3_ffn_in['b2']}

def reference(x, cond_1024, L0_cond_conv_b, L0_cond_Wp, L0_cond_bp, L0_cond_Ws, L0_cond_bs, L0_cond_A_log, L0_cond_dt_log, L0_cond_Wo, L0_cond_bo, L0_ffn_w_freq_real, L0_ffn_w_freq_imag, L0_ffn_bias, L1_cond_W, L1_cond_b, L1_cond_alpha, L1_ffn_w_gate, L1_ffn_w_up, L1_ffn_w_down, L2_cond_W_z, L2_cond_U_z, L2_cond_C_z, L2_cond_b_z, L2_cond_W_r, L2_cond_U_r, L2_cond_C_r, L2_cond_b_r, L2_cond_W, L2_cond_U, L2_cond_C, L2_cond_b, L2_ffn_gate, L2_ffn_gate_up_proj, L2_ffn_down_proj, L3_cond_router_w, L3_cond_router_t_w, L3_cond_router_bias, L3_cond_sw1, L3_cond_sw3, L3_cond_sw2, L3_cond_rw1, L3_cond_rw2, L3_ffn_W1, L3_ffn_b1, L3_ffn_W2, L3_ffn_b2):
    import jax
    import jax.numpy as jnp

    def _L0_cond_ref(x, conv_w, conv_b, Wp, bp, Ws, bs, A_log, dt_log, Wo, bo):
        import jax, jax.numpy as jnp
        import numpy as np
        B, L, D = x.shape
        K = conv_w.shape[0]
        N = Ws.shape[1]
        x_pad = jnp.pad(x, ((0, 0), (K - 1, 0), (0, 0)))
        conv = conv_b + sum((x_pad[:, k:k + L, :] * conv_w[k, 0] for k in range(K)))
        proj = conv @ Wp + bp
        B_t = jax.nn.softplus(proj[..., :N])
        C_t = jnp.tanh(proj[..., N:])
        u = x @ Ws + bs
        A = -jax.nn.softplus(A_log)
        dt = jax.nn.softplus(dt_log)
        decay = 1.0 + dt * A

        def step(state, inputs):
            u_t, b_t, c_t = inputs
            state = decay * state + dt * b_t * u_t
            return (state, c_t * state)
        init = jnp.zeros((B, N), dtype=x.dtype)
        xs = tuple((jnp.swapaxes(a, 0, 1) for a in (u, B_t, C_t)))
        _, ys = jax.lax.scan(step, init, xs, unroll=4)
        y = jnp.swapaxes(ys, 0, 1)
        return y @ Wo + bo

    def _L0_ffn_ref(x, w_freq_real, w_freq_imag, bias):
        import jax, jax.numpy as jnp
        import numpy as np
        B, N, D = (4, 512, 256)
        SPARSITY = 0.01
        w = jax.lax.complex(w_freq_real, w_freq_imag)
        x_freq = jnp.fft.fft(x, axis=-1)
        y_freq = jnp.einsum('bnd,do->bno', x_freq, w)
        y = jnp.real(jnp.fft.ifft(y_freq, axis=-1))
        return y + bias

    def _L1_cond_ref(h_t, z, W, b, alpha):
        import jax, jax.numpy as jnp
        import numpy as np
        LATENT = 256
        D = h_t.shape[-1]
        Wh = W[:, :D]
        Wz = W[:, D:]
        leak = 1.0 - alpha

        def step(h, z_t):
            gate = jax.nn.sigmoid(h @ Wh.T + z_t @ Wz.T + b)
            h_new = jnp.tanh(h * leak + gate * z_t)
            return (h_new, h_new)
        _, hs = jax.lax.scan(step, h_t, jnp.swapaxes(z, 0, 1))
        return jnp.swapaxes(hs, 0, 1)

    def _L1_ffn_ref(x, w_gate, w_up, w_down):
        import jax, jax.numpy as jnp
        import numpy as np
        HIDDEN = 256
        INNER = 1024

        def _weight_quant(w):
            scale = 1.0 / jnp.clip(jnp.mean(jnp.abs(w)), 1e-05)
            wq = jnp.clip(jnp.round(w * scale), -1.0, 1.0) / scale
            return w + jax.lax.stop_gradient(wq - w)

        def _act_quant(x):
            scale = 127.0 / jnp.clip(jnp.max(jnp.abs(x), axis=-1, keepdims=True), 1e-05)
            xq = jnp.clip(jnp.round(x * scale), -128.0, 127.0) / scale
            return x + jax.lax.stop_gradient(xq - x)

        def _bitlinear(x, w):
            return jnp.einsum('bsi,oi->bso', _act_quant(x), _weight_quant(w))
        gate = jax.nn.silu(_bitlinear(x, w_gate))
        up = _bitlinear(x, w_up)
        return _bitlinear(gate * up, w_down)

    def _L2_cond_ref(video, seq, W_z, U_z, C_z, b_z, W_r, U_r, C_r, b_r, W, U, C, b):
        import jax, jax.numpy as jnp
        import numpy as np
        B, T, D_IN, V_IN, E = (64, 128, 256, 256, 256)
        vz = video @ C_z + b_z
        vr = video @ C_r + b_r
        vh = video @ C + b
        xz = jnp.einsum('btd,de->bte', seq, W_z)
        xr = jnp.einsum('btd,de->bte', seq, W_r)
        xh = jnp.einsum('btd,de->bte', seq, W)

        def step(h, xs):
            xzt, xrt, xht = xs
            z = jax.nn.sigmoid(xzt + h @ U_z + vz)
            r = jax.nn.sigmoid(xrt + h @ U_r + vr)
            hh = jnp.tanh(xht + r * h @ U + vh)
            h_new = (1.0 - z) * h + z * hh
            return (h_new, h_new)
        h0 = jnp.zeros((seq.shape[0], U.shape[0]), seq.dtype)
        xs = (jnp.swapaxes(xz, 0, 1), jnp.swapaxes(xr, 0, 1), jnp.swapaxes(xh, 0, 1))
        _, out_t = jax.lax.scan(step, h0, xs)
        return jnp.swapaxes(out_t, 0, 1)

    def _L2_ffn_ref(hidden_states, gate, gate_up_proj, down_proj):
        import jax, jax.numpy as jnp
        import numpy as np
        NUM_EXPERTS = 64
        TOP_K = 8
        HIDDEN = 256
        INTER = 192
        B, S = (2, 512)
        b, s, h = hidden_states.shape
        x = hidden_states.reshape(-1, h)
        router_logits = x @ gate.T
        probs = jax.nn.softmax(router_logits.astype(jnp.float32), axis=-1)
        topk_w, selected = jax.lax.top_k(probs, TOP_K)
        topk_w = topk_w / topk_w.sum(axis=-1, keepdims=True)
        topk_w = topk_w.astype(x.dtype)
        flat_experts = selected.reshape(-1)
        gather_indices = jnp.argsort(flat_experts, stable=True)
        token_counts = jnp.bincount(flat_experts, length=NUM_EXPERTS).astype(jnp.int32)
        x_perm = x[gather_indices // TOP_K]
        first_gemm = jax.lax.ragged_dot(x_perm, jnp.swapaxes(gate_up_proj, 1, 2), token_counts)
        intermediate = jax.nn.silu(first_gemm[:, :INTER]) * first_gemm[:, INTER:]
        second_gemm = jax.lax.ragged_dot(intermediate, jnp.swapaxes(down_proj, 1, 2), token_counts)
        unperm = jnp.zeros_like(second_gemm).at[gather_indices].set(second_gemm)
        out = (unperm.reshape(-1, TOP_K, h) * topk_w[..., None]).sum(axis=1)
        return out.reshape(b, s, h)

    def _L3_cond_ref(x, t_emb, router_w, router_t_w, router_bias, sw1, sw3, sw2, rw1, rw2):
        import jax, jax.numpy as jnp
        import numpy as np
        TOP_K = 2
        N_EXPERTS = 8
        N_SHARED = 1
        EPS = 1e-09
        B, T, C = x.shape
        N = B * T
        x_flat = x.reshape(N, C)
        shared_out = jnp.einsum('nh,dh->nd', jax.nn.silu(x_flat @ sw1.T) * (x_flat @ sw3.T), sw2)
        t_bias = t_emb @ router_t_w.T
        t_bias_flat = jnp.broadcast_to(t_bias[:, None, :], (B, T, N_EXPERTS)).reshape(N, N_EXPERTS)
        s = jax.nn.sigmoid((x_flat @ router_w.T + t_bias_flat).astype(jnp.float32))
        sel_scores = s + router_bias
        _, topk_idx = jax.lax.top_k(sel_scores, TOP_K)
        s_sel = jnp.take_along_axis(s, topk_idx, axis=1)
        denom = jnp.sum(s_sel, axis=1, keepdims=True)
        gates = jnp.where(denom > EPS, s_sel / (denom + EPS), 1.0 / TOP_K).astype(x.dtype)
        combine = jnp.sum(gates[:, :, None] * jax.nn.one_hot(topk_idx, N_EXPERTS, dtype=x.dtype), axis=1)
        H = jax.nn.gelu(jnp.einsum('nd,ehd->enh', x_flat, rw1), approximate=False)
        O = jnp.einsum('enh,edh->end', H, rw2)
        routed_out = jnp.einsum('end,ne->nd', O, combine)
        out = (shared_out + routed_out) / (N_SHARED + TOP_K)
        return out.reshape(B, T, C)

    def _L3_ffn_ref(x, W1, b1, W2, b2):
        import jax, jax.numpy as jnp
        import numpy as np
        QMIN, QMAX = (-128.0, 127.0)

        def _affine_quantize(x):
            amin, amax = (jnp.min(x), jnp.max(x))
            scale = jnp.maximum((amax - amin) / 255.0, 1e-08)
            zp = jnp.clip(jnp.round(-amin / scale) + QMIN, QMIN, QMAX)
            q = jnp.clip(jnp.round(x / scale) + zp, QMIN, QMAX)
            return (q, scale, zp)

        def _sym_quantize(w):
            scale = jnp.maximum(jnp.max(jnp.abs(w)) / 127.0, 1e-08)
            q = jnp.clip(jnp.round(w / scale), -127.0, 127.0)
            return (q, scale)

        def _qlinear(x, W, b):
            xq, sx, zx = _affine_quantize(x)
            wq, sw = _sym_quantize(W)
            acc = jnp.einsum('bsh,oh->bso', xq - zx, wq)
            return acc * (sx * sw) + b
        h = _qlinear(x, W1, b1)
        h = jax.nn.gelu(h, approximate=False)
        out = _qlinear(h, W2, b2)
        return out
    x = x + _L0_ffn_ref(_L0_cond_ref(x, cond_1024[:, None, :], L0_cond_conv_b, L0_cond_Wp, L0_cond_bp, L0_cond_Ws, L0_cond_bs, L0_cond_A_log, L0_cond_dt_log, L0_cond_Wo, L0_cond_bo), L0_ffn_w_freq_real, L0_ffn_w_freq_imag, L0_ffn_bias)
    x = x + _L1_ffn_ref(_L1_cond_ref(cond_1024, x, L1_cond_W, L1_cond_b, L1_cond_alpha), L1_ffn_w_gate, L1_ffn_w_up, L1_ffn_w_down)
    x = x + _L2_ffn_ref(_L2_cond_ref(cond_1024, x, L2_cond_W_z, L2_cond_U_z, L2_cond_C_z, L2_cond_b_z, L2_cond_W_r, L2_cond_U_r, L2_cond_C_r, L2_cond_b_r, L2_cond_W, L2_cond_U, L2_cond_C, L2_cond_b), L2_ffn_gate, L2_ffn_gate_up_proj, L2_ffn_down_proj)
    x = x + _L3_ffn_ref(_L3_cond_ref(x, cond_1024, L3_cond_router_w, L3_cond_router_t_w, L3_cond_router_bias, L3_cond_sw1, L3_cond_sw3, L3_cond_sw2, L3_cond_rw1, L3_cond_rw2), L3_ffn_W1, L3_ffn_b1, L3_ffn_W2, L3_ffn_b2)
    return x

_drawn_inputs = setup_inputs


def setup_inputs(seed=0):
    import zlib

    import numpy as np

    out = dict(_drawn_inputs(seed))
    spreads = {'L0_cond_conv_b': (0.0, 0.1),
     'L0_cond_bp': (0.0, 0.1),
     'L0_cond_bs': (0.0, 0.436),
     'L0_cond_bo': (0.0, 0.1),
     'L1_cond_alpha': (0.10000000149011612, 0.6),
     'L2_cond_b_z': (0.0, 0.8),
     'L2_cond_b_r': (0.0, 0.8),
     'L2_cond_b': (0.0, 0.8),
     'L3_cond_router_bias': (0.0, 0.8)}
    factors = {'L0_cond_A_log': 8.0,
     'L0_cond_dt_log': 8.0,
     'L0_ffn_bias': 5.465,
     'L1_cond_W': 4.802,
     'L1_cond_b': 8.0,
     'L2_cond_W_z': 8.0,
     'L2_cond_U_z': 8.0,
     'L2_cond_C_z': 8.0,
     'L2_cond_W_r': 8.0,
     'L2_cond_U_r': 8.0,
     'L2_cond_C_r': 8.0,
     'L2_cond_W': 8.0,
     'L2_cond_U': 8.0,
     'L2_cond_C': 8.0,
     'L2_ffn_gate': 8.0,
     'L2_ffn_gate_up_proj': 8.0,
     'L2_ffn_down_proj': 8.0,
     'L3_cond_router_w': 8.0,
     'L3_cond_router_t_w': 21.707,
     'L3_cond_sw1': 8.0,
     'L3_cond_sw3': 8.0,
     'L3_cond_sw2': 8.0,
     'L3_cond_rw1': 8.0,
     'L3_cond_rw2': 8.0,
     'L3_ffn_W1': 8.0,
     'L3_ffn_b1': 189.612,
     'L3_ffn_W2': 5.073,
     'L3_ffn_b2': 187.776}
    for name, (base, spread) in spreads.items():
        noise = np.random.default_rng([zlib.crc32(name.encode()), seed]).standard_normal(out[name].shape)
        drawn = base * np.exp(spread * noise) if base else spread * noise
        out[name] = jnp.asarray(drawn.astype(out[name].dtype))
    for name, factor in factors.items():
        out[name] = (out[name] * factor).astype(out[name].dtype)
    return out
```

```python
import numpy as np

import concourse.bass as bass
from concourse import mybir
from contextlib import ExitStack

F32 = mybir.dt.float32
BF16 = mybir.dt.bfloat16
FP16 = mybir.dt.float16
I32 = mybir.dt.int32
U32 = mybir.dt.uint32
ALU = mybir.AluOpType
ACT = mybir.ActivationFunctionType
AXX = mybir.AxisListType.X
RED = bass.bass_isa.ReduceOp

P = 128
B, T, D = 2, 1024, 256
KH = D // P
N = B * T
NS = 64
STEPS = P // B
NCH = T // STEPS
INNER = 1024
BLK = 512
NBLK = N // BLK
ROUND = 1.5 * 2 ** 23
EXP_BITS = 0x7F800000
TOP = 13

NE, TOPK, INTER = 64, 8, 192
REGION = N + P
NROWS = NE * REGION + P
NTILES = N * TOPK // P + NE - 1
NTC = -(-NTILES // P)
E3, H3, S3 = 8, 128, 512


class Unit:

    def __init__(self, eng, sem):
        self.eng, self.sem, self.value, self.seen = eng, sem, 0, {}

    def mark(self, ins):
        ins.then_inc(self.sem, 1)
        self.value += 1
        return (self.sem, self.value)

    def wait(self, *tickets):
        for sem, value in tickets:
            if self.seen.get(sem.name, 0) < value:
                self.eng.wait_ge(sem, value)
                self.seen[sem.name] = value


class Loads:

    def __init__(self, eng, sem):
        self.eng, self.sem, self.value = eng, sem, 0

    def load(self, dst, src):
        self.eng.dma_start(dst, src).then_inc(self.sem, 16)
        self.value += 16

    @property
    def all(self):
        return (self.sem, self.value)


def build_program(nc, A, out):
    with ExitStack() as ctx:
        emit(nc, A, out, ctx)


def emit(nc, A, out, ctx):
    phase = [ctx]

    def sb(name, shape, dt=F32):
        return phase[-1].enter_context(nc.sbuf_tensor(name, shape, dt))[:]

    def begin():
        phase.append(ExitStack())

    def end():
        phase.pop().close()

    def psum(name):
        return ctx.enter_context(nc.psum_tensor(name, [P, BLK], F32))[:]

    def sem(name):
        return ctx.enter_context(nc.semaphore(name))

    pe, act, dve, pool = nc.tensor, nc.scalar, nc.vector, nc.gpsimd
    PE, AC, DV, PO, SP = (Unit(e, sem("done_" + n)) for e, n in
                          ((pe, "pe"), (act, "act"), (dve, "dve"), (pool, "pool"), (nc.sync, "sp")))
    halves = lambda a: a.rearrange("(k p) n -> p k n", p=P)

    bank_g1, bank_z, bank_r, bank_h = (psum("bank_" + n) for n in ("g1", "z", "r", "h"))
    work = [psum(f"work{i}") for i in range(4)]

    ld0 = Loads(nc.sync, sem("loads_layer0"))
    ld1 = Loads(nc.sync, sem("loads_recurrent"))
    ld2 = Loads(nc.sync, sem("loads_ffn1"))

    x = sb("x", [P, KH, T, B])
    xf = x.rearrange("p k t b -> p k (t b)")
    condT = sb("condT", [P, KH, B])
    ident, ones = sb("ident", [P, P]), sb("ones", [P, P])
    ones16, ident16 = sb("ones16", [P, P], BF16), sb("ident16", [P, P], BF16)
    batch_sel = sb("batch_sel", [B, P])
    region_row = sb("region_row", [P, NE])
    chosen_sum = sb("chosen_sum", [P, NE], BF16)
    top = sb("top", [P, NCH, TOPK])
    zero_rows = sb("zero_rows", [P, D])
    feature_cols = sb("feature_cols", [P, 3, KH])
    begin()
    GATES = ("g1", "z", "r", "h")
    rec = {g: sb("rec_" + g, [P, KH, D]) for g in GATES}
    inp = {g: sb("inp_" + g, [P, KH, D]) for g in GATES}
    vid = {g: sb("vid_" + g, [P, KH, D]) for g in GATES[1:]}
    brow = {g: sb("brow_" + g, [1, D]) for g in GATES}
    begin()
    cos, sin = sb("cos", [P, KH, D]), sb("sin", [P, KH, D])
    w_re, w_im = sb("w_re", [P, KH, D]), sb("w_im", [P, KH, D])
    vT = sb("vT", [P, KH, NS + 1])
    conv_b, ffn0_b, alpha = (feature_cols[:, i] for i in range(3))
    wp, ws = sb("wp", [P, KH, 2 * NS]), sb("ws", [P, KH, NS])
    bias0 = sb("bias0", [NS, 5])
    for dst, src in ((cos, halves(A["cos"])), (sin, halves(A["sin"])),
                     (vT, halves(A["WoT_bo"])),
                     (w_re, halves(A["w_re"])), (w_im, halves(A["w_im"])),
                     (condT, halves(A["condT"])), (feature_cols, A["feature_cols"]),
                     (wp, halves(A["Wp"])), (ws, halves(A["Ws"])),
                     (bias0, A["state_cols"]), (ident, A["ident"])):
        ld0.load(dst, src)
    for k in range(KH):
        ld0.load(xf[:, k], A["xT"][k * P:(k + 1) * P])

    for g in GATES:
        ld1.load(rec[g], halves(A["rec_" + g]))
        ld1.load(inp[g], halves(A["inp_" + g]))
        ld1.load(brow[g], A["b_" + g].unsqueeze(0))
    for g in GATES[1:]:
        ld1.load(vid[g], halves(A["vid_" + g]))
    ld1.load(batch_sel, A["batch_sel"])

    ones_ready = DV.mark(dve.memset(ones, 1.0))

    NV = NS + 1
    v1, v2, v2n = (sb(n, [P, KH, NV]) for n in ("v1", "v2", "v2n"))
    a1, a2n = sb("a1", [P, KH, NV]), sb("a2n", [P, KH, NV])
    wom = sb("wom", [NV, D])
    PE.wait(ld0.all)
    for dst_bank, mat in ((work[0], cos), (work[1], sin)):
        for m in range(KH):
            for k in range(KH):
                ins = pe.matmul(dst_bank[:, m * NV:(m + 1) * NV], mat[:, k, m * P:(m + 1) * P], vT[:, k, :],
                                start=(k == 0), stop=(k == KH - 1), skip_group_check=True)
    v_done = PE.mark(ins)
    DV.wait(v_done)
    pv = [w[:, 0:KH * NV].rearrange("p (k n) -> p k n", k=KH) for w in work]
    dve.tensor_copy(v1, pv[0])
    dve.tensor_copy(v2, pv[1])
    v_sb = DV.mark(dve.tensor_scalar(v2n, pv[1], -1.0, None, ALU.mult))
    PE.wait(v_sb)
    for bank, terms in ((work[2], ((w_re, v1), (w_im, v2))), (work[3], ((w_im, v1), (w_re, v2n)))):
        for m in range(KH):
            for j, (mat, v) in enumerate(terms):
                for k in range(KH):
                    ins = pe.matmul(bank[:, m * NV:(m + 1) * NV], mat[:, k, m * P:(m + 1) * P], v[:, k, :],
                                    start=(j == 0 and k == 0), stop=(j == 1 and k == KH - 1),
                                    skip_group_check=True)
    a_done = PE.mark(ins)
    DV.wait(a_done)
    dve.tensor_copy(a1, pv[2])
    a_sb = DV.mark(dve.tensor_scalar(a2n, pv[3], -1.0, None, ALU.mult))
    PE.wait(a_sb)
    for j, (mat, a) in enumerate(((cos, a1), (sin, a2n))):
        for k in range(KH):
            ins = pe.matmul(work[0][0:NV, 0:D], a[:, k, :], mat[:, k, :], start=(j == 0 and k == 0),
                            stop=(j == 1 and k == KH - 1))
    wom_done = PE.mark(ins)
    DV.wait(wom_done)
    wom_sb = DV.mark(dve.tensor_scalar(wom, work[0][0:NV, 0:D], 1.0 / D, None, ALU.mult))

    conv = sb("conv", [P, KH, N])
    DV.wait(ld0.all)
    for k in range(KH):
        c = DV.mark(dve.tensor_scalar(conv[:, k], xf[:, k], condT[:, k, 1:2], conv_b[:, k:k + 1], ALU.mult, ALU.add))
        DV.wait(c)
        conv_done = DV.mark(dve.scalar_tensor_tensor(conv[:, k, B:N], xf[:, k, 0:N - B], condT[:, k, 0:1],
                                                     conv[:, k, B:N], ALU.mult, ALU.add))
    proj = {n: sb("proj_" + n, [NS, N]) for n in ("b", "c", "u")}
    banks0 = [work[1], work[2], work[3], bank_g1, bank_z, bank_r]
    free = {i: None for i in range(6)}
    PE.wait(a_sb)
    n = 0
    for j in range(NBLK):
        cols = slice(j * BLK, (j + 1) * BLK)
        for name, w, src in (("u", ws, xf), ("b", wp[:, :, 0:NS], conv), ("c", wp[:, :, NS:2 * NS], conv)):
            bank = banks0[n % 6]
            if name == "b":
                PE.wait(conv_done)
            if free[n % 6]:
                PE.wait(free[n % 6])
            for k in range(KH):
                ins = pe.matmul(bank[0:NS, :], w[:, k, :], src[:, k, cols], start=(k == 0), stop=(k == KH - 1))
            mm = PE.mark(ins)
            AC.wait(mm)
            col = {"b": 0, "c": 1, "u": 2}[name]
            free[n % 6] = AC.mark(act.activation(proj[name][:, cols], bank[0:NS, :], ACT.Identity,
                                                 bias=bias0[:, col:col + 1]))
            n += 1
    proj_done = free[(n - 1) % 6]

    def softplus(dst, src, tmp, ready):
        AC.wait(ready)
        t = AC.mark(act.activation(tmp, src, ACT.Abs))
        AC.wait(t)
        t = AC.mark(act.activation(tmp, tmp, ACT.Exp, scale=-1.0))
        AC.wait(t)
        t = AC.mark(act.activation(tmp, tmp, ACT.Ln, bias=1.0))
        DV.wait(t)
        return DV.mark(dve.scalar_tensor_tensor(dst, src, 0.0, tmp, ALU.max, ALU.add))

    rates, rates_tmp, decay = sb("rates", [NS, 2]), sb("rates_tmp", [NS, 2]), sb("decay", [NS, 1])
    sp_tmp = conv[0:NS].rearrange("p k n -> p (k n)")
    t = softplus(rates, bias0[:, 3:5], rates_tmp, ld0.all)
    DV.wait(t)
    t = DV.mark(dve.tensor_tensor(decay, rates[:, 0:1], rates[:, 1:2], ALU.mult))
    DV.wait(t)
    decay_done = DV.mark(dve.tensor_scalar(decay, decay, -1.0, 1.0, ALU.mult, ALU.add))
    b_done = softplus(proj["b"], proj["b"], sp_tmp[:, 0:N], proj_done)
    tanh_done = AC.mark(act.activation(proj["c"], proj["c"], ACT.Tanh))
    DV.wait(b_done)
    DV.wait(proj_done)
    drive_done = DV.mark(dve.scalar_tensor_tensor(proj["u"], proj["b"], rates[:, 1:2], proj["u"], ALU.mult, ALU.mult))
    state = sp_tmp[:, N:2 * N].rearrange("p (t b) -> p t b", b=B)
    drive = proj["u"].rearrange("p (t b) -> p t b", b=B)
    DV.wait(drive_done, decay_done)
    for b in range(B):
        scan_done = DV.mark(dve.tensor_tensor_scan(state[:, :, b], decay.to_broadcast([NS, T]), drive[:, :, b],
                                                   0.0, ALU.mult, ALU.add))
    y = sb("y", [NV, N])
    y_ones = DV.mark(dve.memset(y[NS:NV, :], 1.0))
    DV.wait(scan_done, tanh_done)
    y_done = DV.mark(dve.tensor_tensor(y[0:NS, :], sp_tmp[:, N:2 * N], proj["c"], ALU.mult))

    PE.wait(wom_sb, y_ones, y_done)
    x0_done = []
    for j in range(NBLK):
        cols = slice(j * BLK, (j + 1) * BLK)
        for m in range(KH):
            i = (j * KH + m) % 4
            if j * KH + m >= 4:
                PE.wait(x0_done[-4])
            mm = PE.mark(pe.matmul(work[i], wom[:, m * P:(m + 1) * P], y[:, cols], start=True, stop=True))
            DV.wait(mm)
            x0_done.append(DV.mark(dve.scalar_tensor_tensor(xf[:, m, cols], work[i], ffn0_b[:, m:m + 1],
                                                            xf[:, m, cols], ALU.add, ALU.add)))

    end()
    maxes, peak = sb("maxes", [P, 4]), sb("peak", [P, 4])
    DV.wait(ld1.all)
    for i, g in enumerate(GATES):
        t = DV.mark(dve.tensor_reduce(maxes[:, i:i + 1], rec[g].rearrange("p k n -> p (k n)"), AXX, ALU.max,
                                      apply_absolute_value=True))
    PO.wait(t)
    t = PO.mark(pool.partition_all_reduce(peak, maxes, P, RED.max))
    DV.wait(t)
    up, down = sb("scale_up", [P, 4]), sb("scale_down", [P, 4])
    ebits, fbits = sb("ebits", [P, 4], I32), sb("fbits", [P, 4], I32)
    t = DV.mark(dve.tensor_scalar(peak, peak, 2.0 ** -100, None, ALU.max))
    DV.wait(t)
    t = DV.mark(dve.tensor_scalar(ebits, peak.bitcast(I32), EXP_BITS, None, ALU.bitwise_and))
    DV.wait(t)
    t = DV.mark(dve.tensor_scalar(fbits, ebits, -1.0, float((TOP + 254) << 23), ALU.mult, ALU.add))
    t2 = DV.mark(dve.tensor_scalar(ebits, ebits, float(-(TOP << 23)), None, ALU.add))
    DV.wait(t2)
    dve.tensor_copy(up, fbits.bitcast(F32))
    t = DV.mark(dve.tensor_copy(down, ebits.bitcast(F32)))
    DV.wait(t)
    hi = {g: sb("hi_" + g, [P, KH, D], FP16) for g in GATES}
    lo = {g: sb("lo_" + g, [P, KH, D], FP16) for g in GATES}
    split_done = {}

    def split(g):
        s = up[:, GATES.index(g):GATES.index(g) + 1]
        t = DV.mark(dve.tensor_scalar(hi[g], rec[g], s, None, ALU.mult))
        dve.tensor_scalar(inp[g], inp[g], s, None, ALU.mult)
        DV.wait(t)
        t = DV.mark(dve.scalar_tensor_tensor(lo[g], rec[g], s, hi[g], ALU.mult, ALU.subtract))
        if g == "g1":
            DV.wait(t)
            dve.tensor_scalar(rec[g], rec[g], s, None, ALU.mult)
            t = DV.mark(dve.tensor_scalar(brow[g], brow[g], s[0:1], None, ALU.mult))
        split_done[g] = t

    vrow = {g: sb("vrow_" + g, [B, D]) for g in GATES[1:]}
    vrow_done = {}

    def video_bias(i, g):
        PE.wait(ld1.all, ones_ready, x0_done[-1])
        for k in range(KH):
            pe.matmul(work[i][0:B, 0:D], condT[:, k, :], vid[g][:, k, :], start=(k == 0), stop=False)
        mm = PE.mark(pe.matmul(work[i][0:B, 0:D], ones[0:1, 0:B], brow[g], start=False, stop=True))
        DV.wait(mm)
        vrow_done[g] = DV.mark(dve.tensor_scalar(vrow[g], work[i][0:B, 0:D], up[0:B, i + 1:i + 2], None, ALU.mult))

    split("g1")
    leak4 = sb("leak4", [P, KH, B])
    t = DV.mark(dve.tensor_scalar(leak4, alpha.unsqueeze(2).to_broadcast([P, KH, B]), -1.0, 1.0, ALU.mult, ALU.add))
    DV.wait(t)

    w1_f32 = {"gate": sb("w_gate32", [P, KH, INNER]), "up": sb("w_up32", [P, KH, INNER]),
              "down": sb("w_down32", [P, INNER // P, D])}
    SP.wait(x0_done[-1])
    for name in ("gate", "up", "down"):
        ld2.load(w1_f32[name], halves(A["w_" + name]))
    wq = {"gate": sb("wq_gate", [P, KH, INNER], BF16), "up": sb("wq_up", [P, KH, INNER], BF16),
          "down": sb("wq_down", [P, INNER // P, D], BF16)}
    sums, mean, wscale = sb("sums", [P, 3]), sb("mean", [P, 3]), sb("wscale", [P, 3])
    flat = lambda a: a.rearrange("p k n -> p (k n)")
    Q = {}

    def weight_sum(i, name):
        DV.wait(ld2.all)
        Q["sum"] = DV.mark(dve.tensor_reduce(sums[:, i:i + 1], flat(w1_f32[name]), AXX, ALU.add,
                                             apply_absolute_value=True))

    def weight_mean():
        PO.wait(Q["sum"])
        t = PO.mark(pool.partition_all_reduce(mean, sums, P, RED.add))
        DV.wait(t)
        t = DV.mark(dve.tensor_scalar(mean, mean, 1.0 / (D * INNER), 1e-5, ALU.mult, ALU.max))
        DV.wait(t)
        Q["scale"] = DV.mark(dve.reciprocal(wscale, mean))

    def weight_quant(i, name, n):
        w = flat(w1_f32[name])[:, n * INNER:(n + 1) * INNER]
        DV.wait(Q["scale"])
        t = DV.mark(dve.tensor_scalar(w, w, wscale[:, i:i + 1], ROUND, ALU.mult, ALU.add))
        DV.wait(t)
        t = DV.mark(dve.tensor_scalar(w, w, ROUND, 1.0, ALU.subtract, ALU.min))
        DV.wait(t)
        Q["ready"] = DV.mark(dve.tensor_scalar(flat(wq[name])[:, n * INNER:(n + 1) * INNER], w, -1.0, None, ALU.max))

    def setup_items():
        todo = [lambda g=g: split(g) for g in GATES[1:]] + [lambda i=i, g=g: video_bias(i, g) for i, g in enumerate(GATES[1:])]
        names = list(enumerate(("gate", "up", "down")))
        todo += [lambda i=i, n=n: weight_sum(i, n) for i, n in names] + [weight_mean]
        return todo + [lambda i=i, n=n, h=h: weight_quant(i, n, h) for i, n in names for h in range(2)]

    ident16_ready = DV.mark(dve.tensor_copy(ident16, ident))

    gate_cols = lambda bank: bank[:, 0:KH * P].rearrange("p (m t b) -> p m t b", m=KH, b=B)
    g1_pairs = sb("g1_pairs", [P, KH * B, 2])
    z_pairs = [sb(f"z_pairs{i}", [P, STEPS, KH, B, 2]) for i in range(2)]
    arg1 = sb("arg1", [P, KH * B, 2])
    h1 = [sb(f"h1_{i}", [P, KH, STEPS, B]) for i in range(2)]
    h1_hi, h1_lo = sb("h1_hi", [P, KH, B], FP16), sb("h1_lo", [P, KH, B], FP16)
    zg_pairs, hh_pairs = sb("zg_pairs", [P, KH * B, 2]), sb("hh_pairs", [P, KH * B, 2])
    h2 = [sb(f"h2_{i}", [P, STEPS, KH * B, 2]) for i in range(2)]
    h2_hi, h2_lo = sb("h2_hi", [P, KH * B, 2], FP16), sb("h2_lo", [P, KH, B], FP16)
    r_gate, omz = sb("r_gate", [P, KH * B]), sb("omz", [P, KH * B])
    rh, rh_hi, rh_lo = sb("rh", [P, KH * B]), sb("rh_hi", [P, KH, B], FP16), sb("rh_lo", [P, KH, B], FP16)
    down_neg = sb("down_neg", [P, 1])
    dve.memset(g1_pairs, 0.0)
    dve.memset(zg_pairs, 0.0)
    rec_ready = DV.mark(dve.tensor_scalar(down_neg, down[:, 1:2], -1.0, None, ALU.mult))

    S = {"h1": None, "h1_lo": None, "leak": None, "h2": None, "h2_lo": None, "g1_read": None,
         "h_read": None, "z_fill": {}, "h1_chunk": {}, "h1_turned": {}, "x1": {}, "h2_chunk": {}, "h2_free": {}}

    def lay_inputs(bank, g, chunk, bias_rows, bias_cols, waits):
        PE.wait(*waits)
        cols = slice(chunk * P, (chunk + 1) * P)
        for m in range(KH):
            o = bank[:, m * P:(m + 1) * P]
            pe.matmul(o, bias_rows[:, m * P:(m + 1) * P], bias_cols, start=(m == 0), stop=False,
                      skip_group_check=True)
            for k in range(KH):
                ins = pe.matmul(o, inp[g][:, k, m * P:(m + 1) * P], xf[:, k, cols], start=False, stop=False,
                                skip_group_check=True)
        return ins

    def state_products(bank, step, g, s_hi, s_lo, lo_ready):
        o = gate_cols(bank)
        for w in (hi[g], lo[g]):
            for m in range(KH):
                for k in range(KH):
                    pe.matmul(o[:, m, step, :], w[:, k, m * P:(m + 1) * P], s_hi(k), start=False, stop=False,
                              skip_group_check=True)
        PE.wait(lo_ready)
        for m in range(KH):
            for k in range(KH):
                ins = pe.matmul(o[:, m, step, :], hi[g][:, k, m * P:(m + 1) * P], s_lo(k), start=False,
                                stop=True, skip_group_check=True)
        return PE.mark(ins)

    two = lambda a: a.rearrange("p (k b) -> p k b", k=KH)
    h2_hi_v = h2_hi.rearrange("p (k b) two -> p k b two", k=KH)

    def fill_z(chunk):
        if chunk >= 2:
            PO.wait(S["z_last"][chunk - 2])
        PO.wait(x0_done[-1])
        for k in range(KH):
            t = PO.mark(pool.tensor_copy(z_pairs[chunk % 2][:, :, k, :, 0], x[:, k, chunk * STEPS:(chunk + 1) * STEPS, :]))
        S["z_fill"][chunk] = t
    S["z_last"] = {}

    def tick(t1, t2):
        if t1 is not None:
            c1, s1 = divmod(t1, STEPS)
            if s1 == 0:
                waits = [split_done["g1"], rec_ready] + ([S["g1_read"]] if S["g1_read"] else [x0_done[-1]])
                lay_inputs(bank_g1, "g1", c1, brow["g1"], ones[0:1, :], waits)
        if t2 is not None:
            c2, s2 = divmod(t2, STEPS)
            if s2 == 0:
                waits = [S["x1"][c2], *split_done.values(), *vrow_done.values()] + ([S["h_read"]] if S["h_read"] else [])
                for g, bank in (("r", bank_r), ("z", bank_z), ("h", bank_h)):
                    ins = lay_inputs(bank, g, c2, vrow[g], batch_sel, waits)
                laid = PE.mark(ins)
            if t2 > 0:
                hi_s, lo_s = (lambda k: h2_hi_v[:, k, :, 1]), (lambda k: h2_lo[:, k, :])
                PE.wait(S["h2"])
                r_mm = state_products(bank_r, s2, "r", hi_s, lo_s, S["h2_lo"])
                z_mm = state_products(bank_z, s2, "z", hi_s, lo_s, S["h2_lo"])
            else:
                r_mm = z_mm = laid
        if t1 is not None:
            if t1 > 0:
                PE.wait(S["h1"])
                g_mm = state_products(bank_g1, s1, "g1", lambda k: h1_hi[:, k, :], lambda k: h1_lo[:, k, :], S["h1_lo"])
            else:
                for m in range(KH):
                    for k in range(KH):
                        ins = pe.matmul(gate_cols(bank_g1)[:, m, 0, :], rec["g1"][:, k, m * P:(m + 1) * P],
                                        condT[:, k, :], start=False, stop=True, skip_group_check=True)
                g_mm = PE.mark(ins)
        if t2 is not None:
            if t2 > 0:
                AC.wait(r_mm)
                r_done = AC.mark(act.activation(two(r_gate), gate_cols(bank_r)[:, :, s2, :], ACT.Sigmoid, scale=down[:, 2:3]))
            AC.wait(z_mm)
            if S["h2_lo"]:
                AC.wait(S["h2_lo"])
            act.activation(zg_pairs[:, :, 1].rearrange("p (k b) -> p k b", k=KH), gate_cols(bank_z)[:, :, s2, :],
                           ACT.Sigmoid, scale=down[:, 1:2])
            z_done = AC.mark(act.activation(two(omz), gate_cols(bank_z)[:, :, s2, :], ACT.Sigmoid, scale=down_neg))
            if t2 > 0:
                h_prev = h2[(t2 - 1) // STEPS % 2][:, (t2 - 1) % STEPS, :, 1]
                DV.wait(r_done)
                rh_ready = DV.mark(dve.tensor_tensor(rh_hi.rearrange("p k b -> p (k b)"), r_gate, h_prev, ALU.mult))
                t = DV.mark(dve.tensor_tensor(rh, r_gate, h_prev, ALU.mult))
                DV.wait(t)
                rh_lo_ready = DV.mark(dve.tensor_tensor(rh_lo.rearrange("p k b -> p (k b)"), rh,
                                                        rh_hi.rearrange("p k b -> p (k b)"), ALU.subtract))
                PE.wait(rh_ready)
                h_mm = state_products(bank_h, s2, "h", lambda k: rh_hi[:, k, :], lambda k: rh_lo[:, k, :], rh_lo_ready)
                DV.wait(z_done)
                keep = DV.mark(dve.tensor_tensor(hh_pairs[:, :, 1], omz, h_prev, ALU.mult))
            else:
                DV.wait(z_done)
                keep = DV.mark(dve.tensor_scalar(hh_pairs[:, :, 1], omz, 0.0, None, ALU.mult))
                h_mm = laid
        if t1 is not None:
            AC.wait(g_mm)
            if S["h1_scan"]:
                AC.wait(S["h1_scan"])
            S["g1_read"] = AC.mark(act.activation(g1_pairs[:, :, 1].rearrange("p (k b) -> p k b", k=KH),
                                                  gate_cols(bank_g1)[:, :, s1, :], ACT.Sigmoid, scale=down[:, 0:1]))
            zp = z_pairs[c1 % 2]
            if t1 == 0:
                DV.wait(S["z_fill"][0])
                S["leak"] = DV.mark(dve.tensor_tensor(zp[:, 0, :, :, 1], condT, leak4, ALU.mult))
            DV.wait(S["g1_read"], S["leak"])
            if s1 == 0:
                DV.wait(S["z_fill"][c1])
            S["h1_scan"] = DV.mark(dve.tensor_tensor_scan(arg1.rearrange("p c two -> p (c two)"),
                                                          g1_pairs.rearrange("p c two -> p (c two)"),
                                                          zp[:, s1].rearrange("p k b two -> p (k b two)"),
                                                          0.0, ALU.mult, ALU.add))
            S["z_last"][c1] = S["h1_scan"]
        if t2 is not None:
            AC.wait(h_mm)
            S["h_read"] = AC.mark(act.activation(hh_pairs[:, :, 0].rearrange("p (k b) -> p k b", k=KH),
                                                 gate_cols(bank_h)[:, :, s2, :], ACT.Tanh, scale=down[:, 3:4]))
            DV.wait(S["h_read"], keep)
            if s2 == 0 and c2 - 2 in S["h2_free"]:
                DV.wait(S["h2_free"][c2 - 2])
            pairs = (zg_pairs.rearrange("p c two -> p (c two)"), hh_pairs.rearrange("p c two -> p (c two)"))
            S["h2_hi"] = DV.mark(dve.tensor_tensor_scan(h2_hi.rearrange("p c two -> p (c two)"), *pairs, 0.0, ALU.mult, ALU.add))
            h_new = h2[c2 % 2][:, s2]
            S["h2"] = DV.mark(dve.tensor_tensor_scan(h_new.rearrange("p c two -> p (c two)"), *pairs, 0.0, ALU.mult, ALU.add))
            DV.wait(S["h2"])
            S["h2_lo"] = DV.mark(dve.tensor_tensor(h2_lo.rearrange("p k b -> p (k b)"), h_new[:, :, 1], h2_hi[:, :, 1], ALU.subtract))
            S["h2"] = S["h2_hi"]
            S["h2_chunk"][c2] = S["h2_lo"]
        if t1 is not None:
            AC.wait(S["h1_scan"])
            if s1 == 0 and c1 >= 2:
                AC.wait(S["h1_turned"][c1 - 2])
            S["h1"] = AC.mark(act.activation(h1_hi.rearrange("p k b -> p (k b)"), arg1[:, :, 1], ACT.Tanh))
            h_new = h1[c1 % 2][:, :, s1, :]
            h32 = AC.mark(act.activation(h_new, two(arg1[:, :, 1]), ACT.Tanh))
            S["h1_chunk"][c1] = h32
            DV.wait(h32)
            S["h1_lo"] = DV.mark(dve.tensor_tensor(h1_lo, h_new, h1_hi, ALU.subtract))
            if t1 + 1 < T:
                nc1, ns1 = divmod(t1 + 1, STEPS)
                if ns1 == 0 and nc1 >= 2:
                    pass
                S["leak"] = DV.mark(dve.tensor_tensor(z_pairs[nc1 % 2][:, ns1, :, :, 1], h_new, leak4, ALU.mult))
    S["h1_scan"] = None

    q_tmp, q1 = sb("q_tmp", [P, INNER]), sb("q1", [P, D], BF16)
    q1T = sb("q1T", [P, KH, P], BF16)
    tok = {n: sb("tok_" + n, [P, 1]) for n in ("max", "inv", "gate", "up", "max2", "inv2", "down")}
    sig, hmid = sb("sig", [P, BLK]), sb("hmid", [P, INNER])
    q2, q2T = sb("q2", [P, INNER], BF16), sb("q2T", [P, INNER // P, P], BF16)
    o1 = sb("o1", [P, D])

    def token_scale(src_max, inv, t):
        DV.wait(t)
        t = DV.mark(dve.tensor_scalar(src_max, src_max, 1e-5, None, ALU.max))
        DV.wait(t)
        t = DV.mark(dve.reciprocal(inv, src_max))
        DV.wait(t)
        return DV.mark(dve.tensor_scalar(inv, inv, 127.0, None, ALU.mult))

    def factor(dst, mx, i):
        return DV.mark(dve.tensor_scalar(dst, mx, mean[:, i:i + 1], 1.0 / 127.0, ALU.mult, ALU.mult))

    def ffn1_items(c):
        R = {}
        w0, w1_, w2, w3 = work
        h = h1[c % 2]

        def turn():
            PE.wait(S["h1_chunk"][c], S.get("w0_free", x0_done[-1]), *vrow_done.values())
            for k in range(KH):
                ins = pe.transpose(w0[:, k * P:(k + 1) * P], h[:, k].rearrange("p t b -> p (t b)"), ident)
            R["t"] = S["h1_turned"][c] = PE.mark(ins)

        def scale_in():
            DV.wait(R["t"])
            t = DV.mark(dve.tensor_reduce(tok["max"], w0[:, 0:D], AXX, ALU.max, apply_absolute_value=True))
            t = token_scale(tok["max"], tok["inv"], t)
            factor(tok["gate"], tok["max"], 0)
            R["f"] = factor(tok["up"], tok["max"], 1)
            DV.wait(t)

        def quant_in():
            t = S["w0_free"] = DV.mark(dve.tensor_scalar(q_tmp[:, 0:D], w0[:, 0:D], tok["inv"], ROUND, ALU.mult, ALU.add))
            DV.wait(t)
            R["q"] = DV.mark(dve.tensor_scalar(q1, q_tmp[:, 0:D], ROUND, None, ALU.subtract))

        def turn_q():
            PE.wait(R["q"], ident16_ready, S.get("w1_free", x0_done[-1]))
            for k in range(KH):
                ins = pe.transpose(w1_.bitcast(BF16)[:, k * P:(k + 1) * P], q1[:, k * P:(k + 1) * P], ident16)
            R["qt"] = PE.mark(ins)
            AC.wait(R["qt"])
            R["qts"] = S["w1_free"] = AC.mark(act.copy(q1T.rearrange("p k n -> p (k n)"), w1_.bitcast(BF16)[:, 0:D]))

        def gate_up(n):
            cols = slice(n * BLK, (n + 1) * BLK)
            PE.wait(R["qts"], Q["ready"], S.get("w23_free", x0_done[-1]))
            for bank, name in ((w2, "gate"), (w3, "up")):
                for k in range(KH):
                    ins = pe.matmul(bank, q1T[:, k, :], wq[name][:, k, cols], start=(k == 0), stop=(k == KH - 1))
            R["gu"] = PE.mark(ins)
            AC.wait(R["gu"], R["f"])
            if n == 1:
                AC.wait(R["sig_read"])
            elif "sig_free" in S:
                AC.wait(S["sig_free"])
            R["sig"] = AC.mark(act.activation(sig, w2, ACT.Sigmoid, scale=tok["gate"]))

        def mid(n):
            cols = slice(n * BLK, (n + 1) * BLK)
            DV.wait(R["sig"])
            t = DV.mark(dve.scalar_tensor_tensor(sig, w2, tok["gate"], sig, ALU.mult, ALU.mult))
            DV.wait(t)
            R["mid"] = S["w23_free"] = R["sig_read"] = S["sig_free"] = DV.mark(
                dve.scalar_tensor_tensor(hmid[:, cols], w3, tok["up"], sig, ALU.mult, ALU.mult))

        def scale_mid():
            DV.wait(R["mid"])
            t = DV.mark(dve.tensor_reduce(tok["max2"], hmid, AXX, ALU.max, apply_absolute_value=True))
            t = token_scale(tok["max2"], tok["inv2"], t)
            R["f2"] = factor(tok["down"], tok["max2"], 2)
            DV.wait(t)

        def quant_mid(n):
            cols = slice(n * BLK, (n + 1) * BLK)
            t = DV.mark(dve.tensor_scalar(q_tmp[:, cols], hmid[:, cols], tok["inv2"], ROUND, ALU.mult, ALU.add))
            DV.wait(t)
            R["q2"] = DV.mark(dve.tensor_scalar(q2[:, cols], q_tmp[:, cols], ROUND, None, ALU.subtract))

        def turn_mid(n):
            if n == 0:
                PE.wait(R["q2"], S["w1_free"])
            for j in range(4 * n, 4 * n + 4):
                ins = pe.transpose(w1_.bitcast(BF16)[:, j * P:(j + 1) * P], q2[:, j * P:(j + 1) * P], ident16)
            if n == 1:
                R["q2t"] = PE.mark(ins)

        def copy_mid():
            AC.wait(R["q2t"])
            R["q2ts"] = S["w1_free"] = AC.mark(act.copy(q2T.rearrange("p k n -> p (k n)"), w1_.bitcast(BF16)))

        def down_proj(n):
            if n == 0:
                PE.wait(R["q2ts"], S["w0_free"])
            for j in range(4 * n, 4 * n + 4):
                ins = pe.matmul(w0[:, 0:D], q2T[:, j, :], wq["down"][:, j, :], start=(j == 0), stop=(j == 7))
            if n == 1:
                R["dn"] = PE.mark(ins)
                AC.wait(R["dn"], R["f2"])
                R["o1"] = S["w0_free"] = AC.mark(act.activation(o1, w0[:, 0:D], ACT.Copy, scale=tok["down"]))

        def turn_out():
            PE.wait(R["o1"])
            for k in range(KH):
                ins = pe.transpose(w0[:, k * P:(k + 1) * P], o1[:, k * P:(k + 1) * P], ident)
            t = PE.mark(ins)
            DV.wait(t)
            xc = xf[:, :, c * P:(c + 1) * P]
            S["x1"][c] = S["w0_free"] = DV.mark(dve.tensor_tensor(
                xc, xc, w0[:, 0:D].rearrange("p (k n) -> p k n", k=KH), ALU.add))

        return [turn, scale_in, quant_in, turn_q, lambda: gate_up(0), lambda: mid(0), lambda: gate_up(1),
                lambda: mid(1), scale_mid, lambda: quant_mid(0), lambda: quant_mid(1), lambda: turn_mid(0),
                lambda: turn_mid(1), copy_mid, lambda: down_proj(0), lambda: down_proj(1), turn_out]

    logit_w = sb("logit_w", [P, KH, NE])
    before, before32 = sb("before", [P, P], BF16), sb("before32", [P, P])
    expert_iota = sb("expert_iota", [P, NE])
    h2c = [sb(f"h2c{i}", [P, KH, P]) for i in range(2)]
    rows = [sb(f"rows{i}", [P, D]) for i in range(2)]
    logits = sb("logits", [P, NE])
    top_i, top_f = sb("top_i", [P, TOPK], U32), sb("top_f", [P, TOPK])
    pick, pick_row = sb("pick", [P, TOPK, NE]), sb("pick_row", [P, TOPK, NE])
    chosen = sb("chosen", [P, NE], BF16)
    place = sb("place", [P, NE])
    slot_f = sb("slot_f", [P, TOPK])
    slot = [sb(f"slot{i}", [P, TOPK], U32) for i in range(2)]
    dest = sb("dest", [P, NCH, TOPK], U32)
    null_id = sb("null_id", [P, NROWS // P], U32)

    x_rows = nc.dram_tensor("x_rows", (NROWS, D), F32, kind="Internal").ap()
    dest_of = nc.dram_tensor("dest_of", (NROWS, 1), U32, kind="Internal").ap()
    y_rows = nc.dram_tensor("y_rows", (N * TOPK, D), F32, kind="Internal").ap()
    scattered = [sem(f"scattered{i}") for i in range(2)]
    ld3 = Loads(nc.sync, sem("loads_moe"))
    init = Loads(nc.sync, sem("init_moe"))

    def prepare_moe():
        for dst, src in ((logit_w, halves(A["logit_w"])), (expert_iota, A["expert_iota"]),
                         (region_row, A["region_row"]), (dest.rearrange("p c k -> p (c k)"), A["dest"])):
            ld3.load(dst, src)
        ld3.load(before32, A["before"])
        dve.memset(zero_rows, 0.0)
        dve.memset(ones16, 1.0)
        dve.memset(chosen_sum, 0.0)
        filled = DV.mark(dve.memset(null_id, N * TOPK))
        DV.wait(ld3.all)
        R["prep"] = DV.mark(dve.tensor_copy(before, before32))
        SP.wait(filled)
        init.load(dest_of.rearrange("(p n) o -> p (n o)", p=P), null_id)
        init.load(x_rows[NE * REGION:NROWS], zero_rows)
        SP.wait(R["prep"])

    R = {"rows_free": {}, "scat": [0, 0]}

    def front_items(c):
        w, i = work[1], c % 2
        L = {}

        def pack():
            PO.wait(S["h2_chunk"][c])
            if c >= 2:
                PO.wait(R["h2c_read"][c - 2])
            v = h2[i].rearrange("p t (k b) two -> p k t b two", k=KH)
            for k in range(KH):
                t = PO.mark(pool.tensor_copy(h2c[i][:, k].rearrange("p (t b) -> p t b", b=B), v[:, k, :, :, 1]))
            S["h2_free"][c] = L["h2c"] = t

        def score():
            PE.wait(L["h2c"], R["prep"], S["w1_free"])
            for k in range(KH):
                pe.matmul(w[:, 0:NE], h2c[i][:, k], logit_w[:, k], start=(k == 0), stop=(k == KH - 1),
                          skip_group_check=True)
            for k in range(KH):
                ins = pe.transpose(w[:, P + k * P:P + (k + 1) * P], h2c[i][:, k], ident)
            L["score"] = R["h2c_read"][c] = PE.mark(ins)

        def take():
            AC.wait(L["score"])
            AC.wait((scattered[i], R["scat"][i]))
            L["rows"] = AC.mark(act.copy(rows[i], w[:, P:P + D]))
            DV.wait(L["rows"])
            L["logits"] = DV.mark(dve.tensor_copy(logits, w[:, 0:NE]))
            S["w1_free"] = L["logits"]

        def largest():
            DV.wait(L["logits"])
            t = DV.mark(dve.max(top[:, c], logits))
            DV.wait(t)
            t = DV.mark(dve.max_index(top_i, top[:, c], logits))
            DV.wait(t)
            t = DV.mark(dve.tensor_copy(top_f, top_i))
            DV.wait(t)
            L["pick"] = DV.mark(dve.tensor_tensor(pick, expert_iota.unsqueeze(1).to_broadcast([P, TOPK, NE]),
                                                  top_f.unsqueeze(2).to_broadcast([P, TOPK, NE]), ALU.is_equal))

        def choose():
            DV.wait(L["pick"])
            with nc.allow_low_precision(reason="sums of eight zeros and ones, exact in bfloat16"):
                L["chosen"] = DV.mark(dve.tensor_reduce(chosen, pick.rearrange("p k e -> p e k"), AXX, ALU.add))

        def rank():
            PE.wait(L["chosen"], S["w1_free"])
            pe.matmul(w[:, 0:NE], before, chosen, start=True, stop=False)
            t = PE.mark(pe.matmul(w[:, 0:NE], ones16, chosen_sum, start=False, stop=True))
            DV.wait(t)
            S["w1_free"] = t = DV.mark(dve.tensor_tensor(place, w[:, 0:NE], region_row, ALU.add))
            R["chosen_sum"] = DV.mark(dve.tensor_tensor(chosen_sum, chosen_sum, chosen, ALU.add))
            DV.wait(t)
            L["pr"] = DV.mark(dve.tensor_tensor(pick_row, pick, place.unsqueeze(1).to_broadcast([P, TOPK, NE]), ALU.mult))

        def slots():
            DV.wait(L["pr"])
            t = DV.mark(dve.tensor_reduce(slot_f, pick_row, AXX, ALU.add))
            DV.wait(t, (scattered[i], R["scat"][i]))
            L["slot"] = DV.mark(dve.tensor_copy(slot[i], slot_f))

        def scatter(k):
            if k == 0:
                PO.wait(L["slot"], L["rows"], init.all)
            for dst, src in ((x_rows, rows[i]), (dest_of, dest[:, c, k:k + 1])):
                pool.indirect_dma_start(dst, bass.IndirectOffsetOnAxis(ap=slot[i][:, k:k + 1], axis=0), src, None,
                                        bounds_check=NE * REGION - 1, oob_is_err=False).then_inc(scattered[i], 16)
                R["scat"][i] += 16

        return [pack, score, take, largest, choose, rank, slots] + [lambda k=k: scatter(k) for k in range(TOPK)]
    R["h2c_read"] = {}

    LAG = STEPS + 28
    items = []
    for tau in range(T + LAG + STEPS):
        if tau < T and tau % STEPS == 0:
            c = tau // STEPS
            if c == 0:
                fill_z(0)
                items += setup_items()
            if c + 1 < NCH:
                items.append(lambda c=c: fill_z(c + 1))
        if tau == STEPS + 20:
            items.append(prepare_moe)
        if tau and tau % STEPS == 0 and tau // STEPS <= NCH:
            items = ffn1_items(tau // STEPS - 1) + items
        if tau - LAG >= STEPS and (tau - LAG) % STEPS == 0:
            items += front_items((tau - LAG) // STEPS - 1)
        t1, t2 = (tau if tau < T else None), (tau - LAG if LAG <= tau < T + LAG else None)
        if t1 is not None or t2 is not None:
            tick(t1, t2)
        if items:
            items.pop(0)()
        if t1 is None and t2 is None and not items:
            break
    assert not items

    end()
    begin()
    counts, tiles, ends = sb("counts", [P, NE]), sb("tiles", [P, NE]), sb("ends", [P, NE])
    w = work[1]
    PE.wait(R["chosen_sum"], S["w1_free"])
    t = PE.mark(pe.matmul(w[:, 0:NE], ones16, chosen_sum, start=True, stop=True))
    DV.wait(t)
    t = DV.mark(dve.tensor_scalar(tiles, w[:, 0:NE], (P - 1) / 2, 1.0 / P, ALU.add, ALU.mult))
    first_pad = DV.mark(dve.tensor_tensor(counts, w[:, 0:NE], region_row, ALU.add))
    DV.wait(t)
    t = DV.mark(dve.tensor_scalar(tiles, tiles, ROUND, ROUND, ALU.add, ALU.subtract))
    DV.wait(t)
    t = DV.mark(dve.tensor_tensor_scan(ends, ones[:, 0:NE], tiles, 0.0, ALU.mult, ALU.add))
    DV.wait(t)
    full, full_end = sb("full", [P, NTC, NE]), sb("full_end", [P, NTC, NE])
    tile_no = sb("tile_no", [P, NTC])
    n_full, last_end, tile_row = (sb(n, [P, NTC]) for n in ("n_full", "last_end", "tile_row"))
    ld4 = Loads(nc.sync, sem("loads_tiles"))
    ld4.load(tile_no, A["tile_no"])
    DV.wait(ld4.all)
    t = DV.mark(dve.tensor_tensor(full, ends.unsqueeze(1).to_broadcast([P, NTC, NE]),
                                  tile_no.unsqueeze(2).to_broadcast([P, NTC, NE]), ALU.is_le))
    DV.wait(t)
    t = DV.mark(dve.tensor_tensor(full_end, ends.unsqueeze(1).to_broadcast([P, NTC, NE]), full, ALU.mult))
    t2 = DV.mark(dve.tensor_reduce(n_full, full, AXX, ALU.add))
    DV.wait(t)
    t = DV.mark(dve.tensor_reduce(last_end, full_end, AXX, ALU.max))
    DV.wait(t, t2)
    t = DV.mark(dve.tensor_tensor(tile_row, tile_no, last_end, ALU.subtract))
    DV.wait(t)
    t = DV.mark(dve.tensor_scalar(tile_row, tile_row, float(P), None, ALU.mult))
    t2 = DV.mark(dve.tensor_scalar(last_end, n_full, float(REGION), None, ALU.mult))
    DV.wait(t2)
    t = DV.mark(dve.tensor_tensor(tile_row, tile_row, last_end, ALU.add))
    DV.wait(t)
    t = DV.mark(dve.tensor_scalar(tile_row, tile_row, float(NE * REGION), None, ALU.min))
    t2 = DV.mark(dve.tensor_scalar(n_full, n_full, float(NE - 1), None, ALU.min))
    PE.wait(t, t2, first_pad)
    table = sb("table", [1, 2 * NTC * P + NE], I32)
    for j in range(NTC):
        pe.transpose(work[2][0:1, j * P:(j + 1) * P], tile_row[:, j:j + 1], ident)
        t = PE.mark(pe.transpose(work[3][0:1, j * P:(j + 1) * P], n_full[:, j:j + 1], ident))
    DV.wait(t)
    dve.tensor_copy(table[:, 0:NTC * P], work[2][0:1, 0:NTC * P])
    dve.tensor_copy(table[:, NTC * P:2 * NTC * P], work[3][0:1, 0:NTC * P])
    table_ready = DV.mark(dve.tensor_copy(table[:, 2 * NTC * P:], counts[0:1, :]))

    SP.wait(table_ready)
    pads = Loads(nc.sync, sem("pad_rows"))
    SP.wait((scattered[0], R["scat"][0]), (scattered[1], R["scat"][1]))
    for e in range(NE):
        row = nc.sync.value_load(table[:, 2 * NTC * P + e:2 * NTC * P + e + 1], min_val=0, max_val=NE * REGION - P)
        pads.load(x_rows[bass.ds(row, P), :], zero_rows)
    SP.wait(pads.all)

    NB = 6
    HI = INTER // 2
    gu_w = [sb(f"gu_w{i}", [P, KH, 2 * INTER]) for i in range(NB)]
    dn_w = [sb(f"dn_w{i}", [HI, 2, D]) for i in range(NB)]
    xt = [sb(f"xt{i}", [P, D]) for i in range(NB)]
    did = [sb(f"did{i}", [P, 1], U32) for i in range(NB)]
    xtT = [sb(f"xtT{i}", [P, KH, P]) for i in range(2)]
    act_s = [sb(f"act_s{i}", [P, INTER]) for i in range(2)]
    midT = [sb(f"midT{i}", [HI, 2, P]) for i in range(2)]
    yt = [sb(f"yt{i}", [P, D]) for i in range(NB)]
    tile_ld = [Loads(nc.sync, sem(f"tile_loads{i}")) for i in range(NB)]
    y_out = [sem(f"y_out{i}") for i in range(NB)]
    y_sent = [0] * NB
    G = {}
    bT, bG, bM, bY = (bank_g1, work[0]), (bank_z, work[1]), (bank_r, work[2]), (bank_h, work[3])

    def fetch(n):
        i = n % NB
        if n >= NB:
            SP.wait(G["y", n - NB], G["did", n - NB])
        row = nc.sync.value_load(table[:, n:n + 1], min_val=0, max_val=NROWS - P)
        ex = nc.sync.value_load(table[:, NTC * P + n:NTC * P + n + 1], min_val=0, max_val=NE - 1)
        L = tile_ld[i]
        L.load(xt[i], x_rows[bass.ds(row, P), :])
        L.load(did[i], dest_of[bass.ds(row, P), :])
        L.load(gu_w[i], A["gate_up"][bass.ds(ex, 1), :, :].rearrange("e (k p) n -> p (e k) n", p=P))
        L.load(dn_w[i], A["down"][bass.ds(ex, 1), :, :].rearrange("e (k p) n -> p (e k) n", p=HI))
        G["ld", n] = L.all

    def turn_x(n):
        i, bank = n % NB, bT[n % 2]
        PE.wait(G["ld", n])
        if n >= 2:
            PE.wait(G["xT", n - 2])
        for k in range(KH):
            t = pe.transpose(bank[:, k * P:(k + 1) * P], xt[i][:, k * P:(k + 1) * P], ident)
        t = PE.mark(t)
        DV.wait(t)
        G["xT", n] = DV.mark(dve.tensor_copy(xtT[n % 2].rearrange("p k n -> p (k n)"), bank[:, 0:D]))

    def gate_up_products(n):
        i, bank = n % NB, bG[n % 2]
        PE.wait(G["xT", n])
        if n >= 2:
            PE.wait(G["mid", n - 2])
        for k in range(KH):
            t = pe.matmul(bank[:, 0:2 * INTER], xtT[n % 2][:, k], gu_w[i][:, k], start=(k == 0), stop=(k == KH - 1))
        t = PE.mark(t)
        AC.wait(t)
        s = act_s[n % 2]
        if n >= 2:
            AC.wait(G["midT_pe", n - 2])
        t = AC.mark(act.activation(s, bank[:, 0:INTER], ACT.Sigmoid))
        DV.wait(t)
        t = DV.mark(dve.tensor_tensor(s, s, bank[:, 0:INTER], ALU.mult))
        DV.wait(t)
        G["mid", n] = DV.mark(dve.tensor_tensor(s, s, bank[:, INTER:2 * INTER], ALU.mult))

    def turn_mid2(n):
        bank = bM[n % 2]
        PE.wait(G["mid", n])
        if n >= 2:
            PE.wait(G["midT", n - 2])
        for j in range(2):
            t = pe.transpose(bank[0:HI, j * P:(j + 1) * P], act_s[n % 2][:, j * HI:(j + 1) * HI], ident)
        G["midT_pe", n] = t = PE.mark(t)
        AC.wait(t)
        G["midT", n] = AC.mark(act.copy(midT[n % 2].rearrange("p k n -> p (k n)"), bank[0:HI, 0:2 * P]))

    def down_products(n):
        i, bank = n % NB, bY[n % 2]
        PE.wait(G["midT", n])
        if n >= 2:
            PE.wait(G["yt", n - 2])
        for j in range(2):
            t = pe.matmul(bank[:, 0:D], midT[n % 2][:, j], dn_w[i][:, j], start=(j == 0), stop=(j == 1))
        G["y", n] = t = PE.mark(t)
        AC.wait(t)
        if n >= NB:
            AC.wait(G["did", n - NB])
        G["yt", n] = AC.mark(act.copy(yt[i], bank[:, 0:D]))
        PO.wait(G["yt", n], G["ld", n])
        pool.indirect_dma_start(y_rows, bass.IndirectOffsetOnAxis(ap=did[i], axis=0), yt[i], None,
                                bounds_check=N * TOPK - 1, oob_is_err=False).then_inc(y_out[i], 16)
        y_sent[i] += 16
        G["did", n] = (y_out[i], y_sent[i])

    PE.wait(S["g1_read"], S["h_read"], S["h2_chunk"][NCH - 1], table_ready)
    for n in range(NB):
        fetch(n)
    for n in range(NTILES + 3):
        if n < NTILES:
            turn_x(n)
        if 1 <= n <= NTILES:
            gate_up_products(n - 1)
        if 2 <= n <= NTILES + 1:
            turn_mid2(n - 2)
        if n >= 3:
            down_products(n - 3)
            if n - 3 + NB < NTILES:
                fetch(n - 3 + NB)

    end()
    begin()
    wts, wsum = sb("wts", [P, NCH, TOPK]), sb("wsum", [P, NCH])
    yk = [sb(f"yk{i}", [P, TOPK, D]) for i in range(3)]
    acc = [sb(f"acc{i}", [P, D]) for i in range(2)]
    t = DV.mark(dve.tensor_tensor(wts, top, top[:, :, 0:1].to_broadcast([P, NCH, TOPK]), ALU.subtract))
    AC.wait(t)
    t = AC.mark(act.activation(wts, wts, ACT.Exp))
    DV.wait(t)
    t = DV.mark(dve.tensor_reduce(wsum, wts, AXX, ALU.add))
    DV.wait(t)
    t = DV.mark(dve.reciprocal(wsum, wsum))
    DV.wait(t)
    wts_done = DV.mark(dve.tensor_tensor(wts, wts, wsum.unsqueeze(2).to_broadcast([P, NCH, TOPK]), ALU.mult))
    yk_ld = [Loads(nc.sync, sem(f"yk_loads{i}")) for i in range(3)]
    for i in range(NB):
        SP.wait((y_out[i], y_sent[i]))
    yr = y_rows.rearrange("(c p k) d -> c p (k d)", p=P, k=TOPK)
    acc_done = {}
    DV.wait(wts_done)
    for c in range(NCH):
        i = c % 3
        if c >= 3:
            SP.wait(acc_done[c - 3])
        yk_ld[i].load(yk[i].rearrange("p k d -> p (k d)"), yr[c])
        DV.wait(yk_ld[i].all)
        a = acc[c % 2]
        if c >= 2:
            DV.wait(S["acc_read"][c - 2])
        t = DV.mark(dve.tensor_scalar(a, yk[i][:, 0], wts[:, c, 0:1], None, ALU.mult))
        for k in range(1, TOPK):
            DV.wait(t)
            t = DV.mark(dve.scalar_tensor_tensor(a, yk[i][:, k], wts[:, c, k:k + 1], a, ALU.mult, ALU.add))
        acc_done[c] = t
        bank = work[c % 2]
        PE.wait(t)
        if c == 0:
            PE.wait(G["mid", NTILES - 1], G["mid", NTILES - 2])
        if c >= 2:
            PE.wait(S["x2"][c - 2])
        for k in range(KH):
            ins = pe.transpose(bank[:, k * P:(k + 1) * P], a[:, k * P:(k + 1) * P], ident)
        S.setdefault("acc_read", {})[c] = t = PE.mark(ins)
        DV.wait(t)
        xc = xf[:, :, c * P:(c + 1) * P]
        S.setdefault("x2", {})[c] = DV.mark(dve.tensor_tensor(xc, xc, bank[:, 0:D].rearrange("p (k n) -> p k n", k=KH), ALU.add))
    x2_done = S["x2"][NCH - 1]

    end()
    begin()
    y3 = sb("y3", [P, KH, N])
    b1c, b2c = sb("b1c", [P, INNER // P]), sb("b2c", [P, KH])
    begin()
    ld5 = Loads(nc.sync, sem("loads_layer3"))
    router, router_t = sb("router", [P, KH, E3]), sb("router_t", [P, KH, E3])
    bias_row, iota3 = sb("bias_row", [P, E3]), sb("iota3", [P, E3])
    row_sel = sb("row_sel", [E3, E3, P])
    sw1, sw3, sw2 = (sb("sw1", [P, KH, S3]), sb("sw3", [P, KH, S3]), sb("sw2", [P, S3 // P, D]))
    rw1, rw2 = sb("rw1", [P, KH, E3 * H3]), sb("rw2", [P, E3, D])
    SP.wait(x2_done)
    for dst, src in ((router, halves(A["router"])), (router_t, halves(A["router_t"])),
                     (bias_row, A["router_bias"].unsqueeze(0).to_broadcast([P, E3])), (iota3, A["iota3"]),
                     (row_sel, A["row_sel"]), (sw1, halves(A["sw1"])), (sw3, halves(A["sw3"])), (sw2, halves(A["sw2"])),
                     (rw1, halves(A["rw1"])), (rw2, halves(A["rw2"])), (b1c, A["b1"]), (b2c, A["b2"])):
        ld5.load(dst, src)
    tb = sb("tb", [B, E3])
    sc = {n: sb("sc_" + n, [P, NCH, E3]) for n in ("s", "sel", "mask", "oh", "comb")}
    m8, i8, f8 = sb("m8", [P, NCH, E3]), sb("i8", [P, NCH, E3], U32), sb("f8", [P, NCH, E3])
    den, okc, inv3 = sb("den", [P, NCH]), sb("okc", [P, NCH]), sb("inv3", [P, NCH])
    combT = sb("combT", [E3, N])
    w = work[2]
    PE.wait(ld5.all, x2_done, G["midT", NTILES - 1], G["midT", NTILES - 2], G["yt", NTILES - 1], G["yt", NTILES - 2])
    for k in range(KH):
        ins = pe.matmul(w[0:B, P * 2:P * 2 + E3], condT[:, k], router_t[:, k], start=(k == 0), stop=(k == KH - 1))
    t = PE.mark(ins)
    DV.wait(t)
    t = DV.mark(dve.tensor_copy(tb, w[0:B, P * 2:P * 2 + E3]))
    PE.wait(t)
    for c in range(NCH):
        o = w[:, c * E3:(c + 1) * E3]
        pe.matmul(o, batch_sel, tb, start=(c == 0), stop=False, skip_group_check=True)
        for k in range(KH):
            ins = pe.matmul(o, xf[:, k, c * P:(c + 1) * P], router[:, k], start=False, stop=(k == KH - 1), skip_group_check=True)
    t = PE.mark(ins)
    AC.wait(t)
    t = AC.mark(act.activation(sc["s"].rearrange("p c e -> p (c e)"), w[:, 0:NCH * E3], ACT.Sigmoid))
    DV.wait(t)
    t = DV.mark(dve.tensor_tensor(sc["sel"], sc["s"], bias_row.unsqueeze(1).to_broadcast([P, NCH, E3]), ALU.add))
    DV.wait(t)
    for c in range(NCH):
        t = DV.mark(dve.max(m8[:, c], sc["sel"][:, c]))
    DV.wait(t)
    for c in range(NCH):
        t = DV.mark(dve.max_index(i8[:, c], m8[:, c], sc["sel"][:, c]))
    DV.wait(t)
    t = DV.mark(dve.tensor_copy(f8, i8))
    DV.wait(t)
    io = iota3.unsqueeze(1).to_broadcast([P, NCH, E3])
    dve.tensor_tensor(sc["mask"], io, f8[:, :, 0:1].to_broadcast([P, NCH, E3]), ALU.is_equal)
    t = DV.mark(dve.tensor_tensor(sc["oh"], io, f8[:, :, 1:2].to_broadcast([P, NCH, E3]), ALU.is_equal))
    DV.wait(t)
    t = DV.mark(dve.tensor_tensor(sc["mask"], sc["mask"], sc["oh"], ALU.add))
    DV.wait(t)
    t = DV.mark(dve.tensor_tensor(sc["s"], sc["s"], sc["mask"], ALU.mult))
    DV.wait(t)
    t = DV.mark(dve.tensor_reduce(den, sc["s"], AXX, ALU.add))
    DV.wait(t)
    t2 = DV.mark(dve.tensor_scalar(okc, den, 1e-9, None, ALU.is_gt))
    t = DV.mark(dve.tensor_scalar(inv3, den, 1e-9, None, ALU.add))
    DV.wait(t)
    t = DV.mark(dve.reciprocal(inv3, inv3))
    DV.wait(t)
    t = DV.mark(dve.tensor_tensor(inv3, inv3, okc, ALU.mult))
    t2 = DV.mark(dve.tensor_scalar(okc, okc, -0.5, 0.5, ALU.mult, ALU.add))
    DV.wait(t2)
    t = DV.mark(dve.tensor_tensor(sc["s"], sc["s"], inv3.unsqueeze(2).to_broadcast([P, NCH, E3]), ALU.mult))
    t2 = DV.mark(dve.tensor_tensor(sc["mask"], sc["mask"], okc.unsqueeze(2).to_broadcast([P, NCH, E3]), ALU.mult))
    DV.wait(t2)
    comb_done = DV.mark(dve.tensor_tensor(sc["comb"], sc["s"], sc["mask"], ALU.add))
    PE.wait(comb_done)
    for g in range(NCH // 4):
        bank = (bank_z, bank_r)[g % 2]
        if g >= 2:
            PE.wait(R["combT", g - 2])
        for j in range(4):
            t = pe.transpose(bank[0:E3, j * P:(j + 1) * P], sc["comb"][:, 4 * g + j], ident)
        t = PE.mark(t)
        DV.wait(t)
        R["combT", g] = DV.mark(dve.tensor_copy(combT[:, g * BLK:(g + 1) * BLK], bank[0:E3, :]))

    NS3 = S3 // P
    s_in = sb("s_in", [P, NS3, N])
    sg = [sb(f"sg{i}", [P, BLK]) for i in range(2)]
    u = 0
    for j in range(NBLK):
        cols = slice(j * BLK, (j + 1) * BLK)
        for m in range(NS3):
            ba, bb = ((work[0], work[1]), (work[2], work[3]))[u % 2]
            if u >= 2:
                PE.wait(R["s_in", u - 2])
            for bank, wt in ((ba, sw1), (bb, sw3)):
                for k in range(KH):
                    ins = pe.matmul(bank, wt[:, k, m * P:(m + 1) * P], xf[:, k, cols], start=(k == 0), stop=(k == KH - 1))
            t = PE.mark(ins)
            AC.wait(t)
            if u >= 2:
                AC.wait(R["s_in", u - 2])
            t = AC.mark(act.activation(sg[u % 2], ba, ACT.Sigmoid))
            DV.wait(t)
            t = DV.mark(dve.tensor_tensor(sg[u % 2], sg[u % 2], ba, ALU.mult))
            DV.wait(t)
            R["s_in", u] = DV.mark(dve.tensor_tensor(s_in[:, m, cols], sg[u % 2], bb, ALU.mult))
            u += 1
    s_in_done = R["s_in", u - 1]

    he = [sb(f"he{i}", [P, BLK]) for i in range(2)]
    oA = ((bank_g1, bank_z), (bank_r, bank_h))
    ext = sb("ext", [P, 2, NBLK * KH])
    PE.wait(s_in_done, R["combT", 2], R["combT", 3])
    u = 0
    for j in range(NBLK):
        cols = slice(j * BLK, (j + 1) * BLK)
        o2 = oA[j % 2]
        if j >= 2:
            PE.wait(R["y3", j - 2])
        for m in range(KH):
            for k in range(NS3):
                pe.matmul(o2[m], sw2[:, k, m * P:(m + 1) * P], s_in[:, k, cols], start=(k == 0), stop=False,
                          skip_group_check=True)
        pend = None
        for e in range(E3 + 1):
            if e < E3:
                bh, bc = ((work[0], work[1]), (work[2], work[3]))[u % 2]
                if u >= 2:
                    PE.wait(R["he", u - 2])
                for k in range(KH):
                    ins = pe.matmul(bh, rw1[:, k, e * H3:(e + 1) * H3], xf[:, k, cols], start=(k == 0), stop=(k == KH - 1))
                ins = pe.matmul(bc, row_sel[:, e], combT[:, cols], start=True, stop=True)
                t = PE.mark(ins)
                AC.wait(t)
                if u >= 2:
                    AC.wait(R["he_pe", u - 2])
                t = AC.mark(act.activation(he[u % 2], bh, ACT.Gelu))
                DV.wait(t)
                R["he", u] = DV.mark(dve.tensor_tensor(he[u % 2], he[u % 2], bc, ALU.mult))
                u += 1
            if e >= 1:
                v = (u - 2) if e < E3 else (u - 1)
                PE.wait(R["he", v])
                for m in range(KH):
                    ins = pe.matmul(o2[m], rw2[:, e - 1, m * P:(m + 1) * P], he[v % 2], start=False, stop=(e == E3),
                                    skip_group_check=True)
                R["he_pe", v] = t = PE.mark(ins)
        DV.wait(t)
        for m in range(KH):
            t = DV.mark(dve.tensor_scalar(y3[:, m, cols], o2[m], 1.0 / 3.0, None, ALU.mult))
        R["y3", j] = t
    y3_done = t

    end()
    begin()
    NI = INNER // P
    w32 = {"W1": sb("W1_32", [P, KH, INNER]), "W2": sb("W2_32", [P, NI, D])}
    wq3 = {"W1": sb("W1_q", [P, KH, INNER], BF16), "W2": sb("W2_q", [P, NI, D], BF16)}
    ld6 = Loads(nc.sync, sem("loads_ffn3"))
    SP.wait(y3_done)
    for n in w32:
        ld6.load(w32[n], halves(A[n]))
    wm, ws_, wi = sb("wm", [P, 2]), sb("w_scale", [P, 2]), sb("w_inv", [P, 2])
    DV.wait(ld6.all)
    for i, n in enumerate(w32):
        t = DV.mark(dve.tensor_reduce(wm[:, i:i + 1], flat(w32[n]), AXX, ALU.max, apply_absolute_value=True))
    PO.wait(t)
    t = PO.mark(pool.partition_all_reduce(ws_, wm, P, RED.max))
    DV.wait(t)
    t = DV.mark(dve.tensor_scalar(ws_, ws_, 1.0 / 127.0, 1e-8, ALU.mult, ALU.max))
    DV.wait(t)
    t = DV.mark(dve.reciprocal(wi, ws_))
    DV.wait(t)
    for i, n in enumerate(w32):
        wv = flat(w32[n])
        t = DV.mark(dve.tensor_scalar(wv, wv, wi[:, i:i + 1], ROUND, ALU.mult, ALU.add))
        DV.wait(t)
        t = DV.mark(dve.tensor_scalar(wv, wv, ROUND, 127.0, ALU.subtract, ALU.min))
        DV.wait(t)
        wq3_done = DV.mark(dve.tensor_scalar(flat(wq3[n]), wv, -127.0, None, ALU.max))

    def affine(tag, ready):
        am, ar = mm_ext[tag], sb("ar_" + tag, [P, 2])
        PO.wait(ready)
        t = PO.mark(pool.partition_all_reduce(ar, am, P, RED.max))
        scale, inv, zp, lo_, hi_ = (sb(f"{n}_{tag}", [P, 1]) for n in ("scale", "inv", "zp", "qlo", "qhi"))
        DV.wait(t)
        t = DV.mark(dve.tensor_tensor(scale, ar[:, 0:1], ar[:, 1:2], ALU.add))
        DV.wait(t)
        t = DV.mark(dve.tensor_scalar(scale, scale, 1.0 / 255.0, 1e-8, ALU.mult, ALU.max))
        DV.wait(t)
        t = DV.mark(dve.reciprocal(inv, scale))
        DV.wait(t)
        t = DV.mark(dve.tensor_tensor(zp, ar[:, 1:2], inv, ALU.mult))
        DV.wait(t)
        t = DV.mark(dve.tensor_scalar(zp, zp, ROUND, ROUND, ALU.add, ALU.subtract))
        DV.wait(t)
        t = DV.mark(dve.tensor_scalar(zp, zp, -128.0, -128.0, ALU.add, ALU.max))
        DV.wait(t)
        t = DV.mark(dve.tensor_scalar(zp, zp, 127.0, None, ALU.min))
        DV.wait(t)
        dve.tensor_scalar(lo_, zp, -1.0, -128.0, ALU.mult, ALU.add)
        t = DV.mark(dve.tensor_scalar(hi_, zp, -1.0, 127.0, ALU.mult, ALU.add))
        return scale, inv, lo_, hi_, t

    mm_ext = {"x": sb("ext_x", [P, 2]), "h": sb("ext_h", [P, 2])}
    fl = flat(y3)
    DV.wait(y3_done)
    dve.tensor_reduce(mm_ext["x"][:, 0:1], fl, AXX, ALU.max)
    t = DV.mark(dve.tensor_reduce(mm_ext["x"][:, 1:2], fl, AXX, ALU.min, negate=True))
    xs, xi, xlo, xhi, t = affine("x", t)
    xq = sb("xq", [P, KH, N], BF16)
    DV.wait(t)
    t = DV.mark(dve.tensor_scalar(fl, fl, xi, ROUND, ALU.mult, ALU.add))
    DV.wait(t)
    t = DV.mark(dve.tensor_scalar(fl, fl, ROUND, xlo, ALU.subtract, ALU.max))
    DV.wait(t)
    xq_done = DV.mark(dve.tensor_scalar(flat(xq), fl, xhi, None, ALU.min))
    f1, f2 = sb("f1", [P, 1]), sb("f2", [P, 1])
    t = DV.mark(dve.tensor_tensor(f1, xs, ws_[:, 0:1], ALU.mult))
    AC.wait(t)
    PE.wait(xq_done, wq3_done)
    h3 = sb("h3", [P, NI, N])
    part = sb("part", [P, 2, NI * NBLK])
    banks = work + [bank_g1, bank_z]
    for v in range(NI * NBLK):
        m, j = divmod(v, NBLK)
        cols = slice(j * BLK, (j + 1) * BLK)
        if v >= 6:
            PE.wait(R["h3", v - 6])
        else:
            PE.wait(R["he", E3 * NBLK - 1], y3_done)
        for k in range(KH):
            ins = pe.matmul(banks[v % 6], wq3["W1"][:, k, m * P:(m + 1) * P], xq[:, k, cols], start=(k == 0), stop=(k == KH - 1))
        t = PE.mark(ins)
        AC.wait(t)
        R["h3", v] = t = AC.mark(act.activation(h3[:, m, cols], banks[v % 6], ACT.Gelu, bias=b1c[:, m:m + 1], scale=f1))
        DV.wait(t)
        dve.tensor_reduce(part[:, 0, v:v + 1], h3[:, m, cols], AXX, ALU.max)
        t = DV.mark(dve.tensor_reduce(part[:, 1, v:v + 1], h3[:, m, cols], AXX, ALU.min, negate=True))
    DV.wait(t)
    t = DV.mark(dve.tensor_reduce(mm_ext["h"], part, AXX, ALU.max))
    hs, hinv, hlo, hhi, t = affine("h", t)
    hq = sb("hq", [P, NI, N], BF16)
    DV.wait(t)
    t = DV.mark(dve.tensor_tensor(f2, hs, ws_[:, 1:2], ALU.mult))
    AC.wait(t)
    for j in range(NBLK):
        cols = slice(j * BLK, (j + 1) * BLK)
        t = DV.mark(dve.tensor_scalar(h3[:, :, cols], h3[:, :, cols], hinv, ROUND, ALU.mult, ALU.add))
        DV.wait(t)
        t = DV.mark(dve.tensor_scalar(h3[:, :, cols], h3[:, :, cols], ROUND, hlo, ALU.subtract, ALU.max))
        DV.wait(t)
        R["hq", j] = DV.mark(dve.tensor_scalar(hq[:, :, cols], h3[:, :, cols], hhi, None, ALU.min))
    o3 = [sb(f"o3_{i}", [P, BLK]) for i in range(2)]
    stores = Loads(nc.sync, sem("stores"))
    for j in range(NBLK):
        cols = slice(j * BLK, (j + 1) * BLK)
        for m in range(KH):
            v = j * KH + m
            PE.wait(R["hq", j], R["h3", NI * NBLK - 1] if v < 2 else R["o3", v - 2])
            for k in range(NI):
                ins = pe.matmul(work[v % 2], wq3["W2"][:, k, m * P:(m + 1) * P], hq[:, k, cols], start=(k == 0), stop=(k == NI - 1))
            t = PE.mark(ins)
            AC.wait(t)
            if v >= 2:
                AC.wait(R["xo", v - 2])
            R["o3", v] = t = AC.mark(act.activation(o3[v % 2], work[v % 2], ACT.Identity, bias=b2c[:, m:m + 1], scale=f2))
            DV.wait(t)
            R["xo", v] = t = DV.mark(dve.tensor_tensor(xf[:, m, cols], xf[:, m, cols], o3[v % 2], ALU.add))
            SP.wait(t)
            stores.load(out[m * P:(m + 1) * P, cols], xf[:, m, cols])
    SP.wait(stores.all)
    end()
    end()


def constants():
    f = np.arange(D)
    angle = 2 * np.pi * ((f[:, None] * f[None, :]) % D) / D
    token_batch = np.arange(P) % B
    return {
        "cos": np.cos(angle).astype(np.float32), "sin": np.sin(angle).astype(np.float32),
        "ident": np.eye(P, dtype=np.float32),
        "before": (f[:P, None] < f[None, :P]).astype(np.float32),
        "expert_iota": np.tile(np.arange(NE, dtype=np.float32), (P, 1)),
        "region_row": np.tile(np.arange(NE, dtype=np.float32) * REGION, (P, 1)),
        "dest": ((np.arange(P)[:, None, None] + P * np.arange(NCH)[None, :, None]) * TOPK
                 + np.arange(TOPK)[None, None, :]).reshape(P, NCH * TOPK).astype(np.uint32),
        "tile_no": (np.arange(P)[:, None] + P * np.arange(NTC)[None, :]).astype(np.float32),
        "iota3": np.tile(np.arange(E3, dtype=np.float32), (P, 1)),
        "row_sel": np.repeat(np.eye(E3, dtype=np.float32)[:, :, None], P, axis=2),
        "batch_sel": (token_batch[None, :] == np.arange(B)[:, None]).astype(np.float32),
    }


def lay_out(inputs):
    a = {n: np.asarray(v) for n, v in inputs.items()}
    t = lambda v: np.ascontiguousarray(np.swapaxes(v, -1, -2))
    out = {
        "xT": np.ascontiguousarray(a["x"].transpose(2, 1, 0)).reshape(D, N),
        "condT": t(a["cond_1024"]), "Wp": a["L0_cond_Wp"], "Ws": a["L0_cond_Ws"],
        "WoT_bo": np.concatenate([t(a["L0_cond_Wo"]), a["L0_cond_bo"][:, None]], axis=1),
        "w_re": a["L0_ffn_w_freq_real"], "w_im": a["L0_ffn_w_freq_imag"],
        "feature_cols": np.ascontiguousarray(np.stack(
            [a[n].reshape(KH, P) for n in ("L0_cond_conv_b", "L0_ffn_bias", "L1_cond_alpha")]).transpose(2, 0, 1)),
        "state_cols": np.stack([a["L0_cond_bp"][:NS], a["L0_cond_bp"][NS:], a["L0_cond_bs"],
                                a["L0_cond_A_log"], a["L0_cond_dt_log"]], axis=1),
        "rec_g1": t(a["L1_cond_W"][:, :D]), "inp_g1": t(a["L1_cond_W"][:, D:]), "b_g1": a["L1_cond_b"],
        "w_gate": t(a["L1_ffn_w_gate"]), "w_up": t(a["L1_ffn_w_up"]), "w_down": t(a["L1_ffn_w_down"]),
        "rec_z": a["L2_cond_U_z"], "inp_z": a["L2_cond_W_z"], "vid_z": a["L2_cond_C_z"], "b_z": a["L2_cond_b_z"],
        "rec_r": a["L2_cond_U_r"], "inp_r": a["L2_cond_W_r"], "vid_r": a["L2_cond_C_r"], "b_r": a["L2_cond_b_r"],
        "rec_h": a["L2_cond_U"], "inp_h": a["L2_cond_W"], "vid_h": a["L2_cond_C"], "b_h": a["L2_cond_b"],
        "logit_w": t(a["L2_ffn_gate"]), "gate_up": t(a["L2_ffn_gate_up_proj"]), "down": t(a["L2_ffn_down_proj"]),
        "router": t(a["L3_cond_router_w"]), "router_t": t(a["L3_cond_router_t_w"]),
        "router_bias": a["L3_cond_router_bias"],
        "sw1": t(a["L3_cond_sw1"]), "sw3": t(a["L3_cond_sw3"]), "sw2": t(a["L3_cond_sw2"]),
        "rw1": np.ascontiguousarray(a["L3_cond_rw1"].transpose(2, 0, 1)).reshape(D, E3 * H3),
        "rw2": np.ascontiguousarray(a["L3_cond_rw2"].transpose(0, 2, 1)).reshape(E3 * H3, D),
        "W1": t(a["L3_ffn_W1"]), "W2": t(a["L3_ffn_W2"]),
        "b1": t(a["L3_ffn_b1"].reshape(INNER // P, P)), "b2": t(a["L3_ffn_b2"].reshape(KH, P)),
    }
    out.update(constants())
    return out


def kernel(**inputs):
    import concourse.bacc as bacc
    from concourse.bass_utils import run_bass_kernel_spmd

    arrays = lay_out(inputs)
    nc = bacc.Bacc("TRN2", target_bir_lowering=False, num_devices=1)
    aps = {n: nc.dram_tensor("in_" + n, a.shape, mybir.dt.from_np(a.dtype), kind="ExternalInput").ap()
           for n, a in arrays.items()}
    out = nc.dram_tensor("out", (D, N), F32, kind="ExternalOutput").ap()
    build_program(nc, aps, out)
    r = run_bass_kernel_spmd(nc, [{"in_" + n: a for n, a in arrays.items()}], core_ids=[0])
    got = r.results[0]["out"]
    return np.ascontiguousarray(got.reshape(D, T, B).transpose(2, 1, 0))
```
